# Optimizing a Trainium2 kernel written in Bass

```python
import numpy as np
import jax
import jax.numpy as jnp

def _softmax(x, axis=-1):
    return jax.nn.softmax(x, axis=axis)

def _gelu(x):
    return jax.nn.gelu(x, approximate=True)

def _silu(x):
    return jax.nn.silu(x)

def _sigmoid(x):
    return jax.nn.sigmoid(x)

def _layernorm(x, axis=-1, eps=1e-05):
    m = jnp.mean(x, axis=axis, keepdims=True)
    v = jnp.var(x, axis=axis, keepdims=True)
    return (x - m) / jnp.sqrt(v + eps)

def _scatter_add(tgt, idx, src, axis=0):
    return tgt.at[idx].add(src)

def _segment_sum(src, seg, n):
    return jax.ops.segment_sum(src, seg, n)
kernel_name = 'mk_cond_resid_d2_seqx_r2_f69f0a'

def setup_inputs(seed: int=0):
    np.random.seed(seed)
    _w = jnp.asarray

    def _rec_inputs():
        import jax
        import jax.numpy as jnp
        _rk = jax.random.key(seed)
        x = 7.22e-05 + 1 * jax.random.normal(jax.random.fold_in(_rk, 1), (128, 128, 512), jnp.float32)
        _lenS = 128 - jax.random.randint(jax.random.fold_in(_rk, 7), (128,), 0, max(1, 128 // 4) + 1, jnp.int32)
        _lenS2 = 128 - jax.random.randint(jax.random.fold_in(_rk, 8), (128,), 0, max(1, 128 // 4) + 1, jnp.int32)
        cond_512 = 0.0061147 + 1.02565 * jax.random.normal(jax.random.fold_in(_rk, 11), (128, 256), jnp.float32)
        return (x, cond_512)
    x, cond_512 = _rec_inputs()

    def _L0_cond_setup():
        import jax, jax.numpy as jnp
        import numpy as np
        import math
        HEAD_NUM = 16
        EPS = 1e-08

        def modulated_linear(x, s, aff_w, aff_b, w, b):
            style = s @ aff_w.T + aff_b
            w_mod = w[None, :, :] * style[:, None, :]
            demod = jax.lax.rsqrt(jnp.sum(w_mod * w_mod, axis=2) + EPS)
            w_mod = w_mod * demod[:, :, None]
            return jnp.einsum('bni,boi->bno', x, w_mod) + b
        key = jax.random.key(seed)
        ks = jax.random.split(key, 6)
        B, N, F, S = (8, 512, 512, 256)
        return {'x': jax.random.normal(ks[0], (B, N, F), dtype=jnp.float32), 's': jax.random.normal(ks[1], (B, S), dtype=jnp.float32), 'k_aff_w': jax.random.normal(ks[2], (F, S), dtype=jnp.float32) * 0.02, 'k_aff_b': jnp.ones((F,), dtype=jnp.float32), 'k_w': jax.random.normal(ks[3], (F, F), dtype=jnp.float32) * 0.02, 'k_b': jnp.zeros((F,), dtype=jnp.float32), 'o_aff_w': jax.random.normal(ks[4], (F, S), dtype=jnp.float32) * 0.02, 'o_aff_b': jnp.ones((F,), dtype=jnp.float32), 'o_w': jax.random.normal(ks[5], (F, F), dtype=jnp.float32) * 0.02, 'o_b': jnp.zeros((F,), dtype=jnp.float32)}
    _L0_cond_all = _L0_cond_setup()
    _L0_cond_in = {k: v for k, v in _L0_cond_all.items() if k in ('k_aff_w', 'k_aff_b', 'k_w', 'k_b', 'o_aff_w', 'o_aff_b', 'o_w', 'o_b')}
    del _L0_cond_all

    def _L1_cond_setup():
        import jax, jax.numpy as jnp
        import numpy as np
        W_DIM = 256
        CLAMP = 256.0
        key = jax.random.key(seed)
        ks = jax.random.split(key, 6)
        B, L, C = (8, 4096, 512)
        return {'x': jax.random.normal(ks[0], (B, L, C), dtype=jnp.float32), 'w': jax.random.normal(ks[1], (B, W_DIM), dtype=jnp.float32), 'weight': jax.random.normal(ks[2], (C, C), dtype=jnp.float32), 'bias': jax.random.normal(ks[3], (C,), dtype=jnp.float32), 'affine_w': jax.random.normal(ks[4], (C, W_DIM), dtype=jnp.float32), 'affine_b': jnp.ones((C,), dtype=jnp.float32)}
    _L1_cond_all = _L1_cond_setup()
    _L1_cond_in = {k: v for k, v in _L1_cond_all.items() if k in ('weight', 'bias', 'affine_w', 'affine_b')}
    del _L1_cond_all
    return {'x': x, 'cond_512': cond_512, 'L0_cond_k_aff_w': _L0_cond_in['k_aff_w'], 'L0_cond_k_aff_b': _L0_cond_in['k_aff_b'], 'L0_cond_k_w': _L0_cond_in['k_w'], 'L0_cond_k_b': _L0_cond_in['k_b'], 'L0_cond_o_aff_w': _L0_cond_in['o_aff_w'], 'L0_cond_o_aff_b': _L0_cond_in['o_aff_b'], 'L0_cond_o_w': _L0_cond_in['o_w'], 'L0_cond_o_b': _L0_cond_in['o_b'], 'L1_cond_weight': _L1_cond_in['weight'], 'L1_cond_bias': _L1_cond_in['bias'], 'L1_cond_affine_w': _L1_cond_in['affine_w'], 'L1_cond_affine_b': _L1_cond_in['affine_b']}

def reference(x, cond_512, L0_cond_k_aff_w, L0_cond_k_aff_b, L0_cond_k_w, L0_cond_k_b, L0_cond_o_aff_w, L0_cond_o_aff_b, L0_cond_o_w, L0_cond_o_b, L1_cond_weight, L1_cond_bias, L1_cond_affine_w, L1_cond_affine_b):
    import jax
    import jax.numpy as jnp

    def _L0_cond_ref(x, s, k_aff_w, k_aff_b, k_w, k_b, o_aff_w, o_aff_b, o_w, o_b):
        import jax, jax.numpy as jnp
        import numpy as np
        import math
        HEAD_NUM = 16
        EPS = 1e-08

        def modulated_linear(x, s, aff_w, aff_b, w, b):
            style = s @ aff_w.T + aff_b
            w_mod = w[None, :, :] * style[:, None, :]
            demod = jax.lax.rsqrt(jnp.sum(w_mod * w_mod, axis=2) + EPS)
            w_mod = w_mod * demod[:, :, None]
            return jnp.einsum('bni,boi->bno', x, w_mod) + b
        B, N, F = x.shape
        H = HEAD_NUM
        D = F // H
        kx = modulated_linear(x, s, k_aff_w, k_aff_b, k_w, k_b)
        kx = kx.reshape(B, N, H, D)
        q = k = v = kx
        scores = jnp.einsum('bnhd,bnjd->bnhj', q, k) / math.sqrt(D)
        A = jax.nn.softmax(scores, axis=-1)
        out = jnp.einsum('bnhj,bnjd->bnhd', A, v).reshape(B, N, F)
        out = modulated_linear(out, s, o_aff_w, o_aff_b, o_w, o_b)
        return out

    def _L1_cond_ref(x, w, weight, bias, affine_w, affine_b):
        import jax, jax.numpy as jnp
        import numpy as np
        W_DIM = 256
        CLAMP = 256.0
        B, L, C = x.shape
        gain = 1.0 / np.sqrt(W_DIM).astype(np.float32)
        styles = w @ (affine_w * gain).T + affine_b
        ws = weight[None, :, :] * styles[:, None, :]
        dcoefs = jax.lax.rsqrt(jnp.sum(ws * ws, axis=2) + 1e-08)
        xm = x * styles[:, None, :]
        y = jnp.einsum('blc,oc->blo', xm, weight)
        y = y * dcoefs[:, None, :]
        y = jnp.clip(y + bias, -CLAMP, CLAMP)
        return y
    x = x + _L0_cond_ref(x, cond_512, L0_cond_k_aff_w, L0_cond_k_aff_b, L0_cond_k_w, L0_cond_k_b, L0_cond_o_aff_w, L0_cond_o_aff_b, L0_cond_o_w, L0_cond_o_b)
    x = x + _L1_cond_ref(x, cond_512, L1_cond_weight, L1_cond_bias, L1_cond_affine_w, L1_cond_affine_b)
    return x

_drawn_inputs = setup_inputs


def setup_inputs(seed=0):
    import zlib

    import numpy as np

    out = dict(_drawn_inputs(seed))
    spreads = {'L0_cond_k_aff_b': (1.0, 0.2),
     'L0_cond_k_b': (0.0, 0.1),
     'L0_cond_o_aff_b': (1.0, 0.2),
     'L0_cond_o_b': (0.0, 0.1),
     'L1_cond_affine_b': (1.0, 0.2)}
    factors = {}
    for name, (base, spread) in spreads.items():
        noise = np.random.default_rng([zlib.crc32(name.encode()), seed]).standard_normal(out[name].shape)
        drawn = base * np.exp(spread * noise) if base else spread * noise
        out[name] = jnp.asarray(drawn.astype(out[name].dtype))
    for name, factor in factors.items():
        out[name] = (out[name] * factor).astype(out[name].dtype)
    return out
```

```python
from contextlib import ExitStack

import concourse.bass as bass
from concourse import mybir

F32 = mybir.dt.float32
F32R = mybir.dt.float32r
BF16 = mybir.dt.bfloat16
ALU = mybir.AluOpType
ACT = mybir.ActivationFunctionType
AX_X = mybir.AxisListType.X

P = 128
HD = 32
EPS = 1e-8
CLAMP = 256.0
MASKED = -1e30

K_STYLE, O_STYLE, L_STYLE, K_DEMOD, O_DEMOD, L_DEMOD = range(6)
K_MAT, O_MAT, L_MAT = range(3)

BANK_X = (0, 1, 0, 1)
BANK_K = (1, 1, 1, 0)
BANK_KN = (1, 0, 1, 0)
BANK_ITEMS = (1, 1, 0, 1)
BANK_ATTN = (0, 1, 0, 0)
BANK_O = (0, 1, 1, 0)
BANK_L = (0, 0, 0, 1)
BANK_OUT = (0, 1, 0, 1)


def modulated_chain_kernel(nc, x, cond, k_aff_w, k_aff_b, k_w, k_b, o_aff_w, o_aff_b, o_w, o_b,
                           l_w, l_b, l_aff_w, l_aff_b, out):
    B, N, F = x.shape
    S = cond.shape[1]
    C = F // P
    GB = 512 // N
    G = B // GB
    SC = S // P
    H = F // HD
    ROWS = P // HD
    Q = 4
    TOK = HD // Q
    U = 2
    SCALE = 1.0 / float(HD) ** 0.5
    GAIN = 1.0 / float(S) ** 0.5
    assert N == P and B == P and C == 4 and GB == 4 and ROWS == 4 and G % 2 == 0
    assert HD == 32 and TOK * H == P

    with ExitStack() as ctx:
        def sb(name, shape, dt=F32):
            return ctx.enter_context(nc.sbuf_tensor(name, shape, dt))

        def sem(name):
            return ctx.enter_context(nc.semaphore(name))

        w_high = [sb(f"w_high{m}", [P, C, F], F32R) for m in range(3)]
        w_low = [sb(f"w_low{m}", [P, C, F], F32R) for m in range(3)]
        mods = sb("mods", [P, 6, C, B])
        bias = sb("bias", [P, 6, C])
        ident = sb("ident", [P, P])
        ones = sb("ones", [P, HD])
        ones_r = sb("ones_r", [2, P], F32R)
        same_lhs = sb("same_lhs", [P, 1, TOK, H], BF16)
        same_rhs = sb("same_rhs", [P, Q, TOK, H], BF16)

        x_in = sb("x_in", [P, GB, F])
        x_res = [sb(f"x_res{p}", [P, C, GB, N]) for p in range(2)]
        xm = sb("xm", [P, 2, GB * N])
        xm_high = sb("xm_high", [P, C, GB * N], F32R)
        xm_low = sb("xm_low", [P, C, GB * N], F32R)
        keys = sb("keys", [P, C, GB, N])
        keys_strip = sb("keys_strip", [P, GB, 32, H])
        keys_item = sb("keys_item", [P, Q, P])
        row_max = sb("row_max", [P, 16])
        max_parts = sb("max_parts", [P, 32], F32R)
        max_blocks = sb("max_blocks", [P, 32])
        max_rows = sb("max_rows", [2, 16, N], F32R)
        probs = sb("probs", [P, ROWS, Q, P])
        attn_nat = sb("attn_nat", [P, H, HD])
        sum_nat = sb("sum_nat", [P, H, HD])
        sum_inv = sb("sum_inv", [P, H])
        attn = sb("attn", [P, C, N])
        attn_high = sb("attn_high", [P, C, GB, N], F32R)
        attn_low = sb("attn_low", [P, C, GB, N], F32R)
        x1 = sb("x1", [P, C, GB, N])
        x1m = sb("x1m", [P, 2, GB * N])
        x1m_high = sb("x1m_high", [P, C, GB * N], F32R)
        x1m_low = sb("x1m_low", [P, C, GB * N], F32R)
        y = sb("y", [P, 2, GB, N])
        x_out = sb("x_out", [P, 2, F])

        ps_scores = ctx.enter_context(nc.psum_tensor("ps_scores", [P, ROWS, Q * P], F32))
        ps_attn = ctx.enter_context(nc.psum_tensor("ps_attn", [P, Q, P], F32))
        ps_sum = ctx.enter_context(nc.psum_tensor("ps_sum", [P, Q, P], F32))
        ps_gen = [ctx.enter_context(nc.psum_tensor(f"ps_gen{i}", [P, 512], F32)) for i in range(2)]

        small_loaded = sem("small_loaded")
        aff_loaded = [sem(f"aff_loaded{m}") for m in range(3)]
        w_loaded = [sem(f"w_loaded{m}") for m in range(3)]
        const_step = sem("const_step")
        ones_made = sem("ones_made")
        small_turned = sem("small_turned")
        small_kept = sem("small_kept")
        aff_turned = sem("aff_turned")
        aff_kept = sem("aff_kept")
        style_summed = sem("style_summed")
        style_made = sem("style_made")
        style_squared = sem("style_squared")
        w_turned = sem("w_turned")
        w_high_made = sem("w_high_made")
        w_low_made = sem("w_low_made")
        w_squared = sem("w_squared")
        norm_summed = sem("norm_summed")
        norm_kept = sem("norm_kept")
        norm_step = sem("norm_step")
        root_made = sem("root_made")
        mods_ready = sem("mods_ready")

        x_loaded = sem("x_loaded")
        x_turned = sem("x_turned")
        xm_made = sem("xm_made")
        x_res_made = sem("x_res_made")
        xm_high_made = sem("xm_high_made")
        xm_low_made = sem("xm_low_made")
        keys_summed = sem("keys_summed")
        keys_made = sem("keys_made")
        keys_turned = sem("keys_turned")
        keys_strip_made = sem("keys_strip_made")
        items_turned = sem("items_turned")
        keys_item_made = sem("keys_item_made")
        scores_ready = [sem(f"scores_ready{u}") for u in range(U)]
        half_max_made = sem("half_max_made")
        max_high_made = sem("max_high_made")
        max_parts_made = sem("max_parts_made")
        max_turned = sem("max_turned")
        max_rows_loaded = sem("max_rows_loaded")
        shifted = [sem(f"shifted{u}") for u in range(U)]
        probs_made = [sem(f"probs_made{u}") for u in range(U)]
        attn_summed = sem("attn_summed")
        attn_nat_made = sem("attn_nat_made")
        sum_nat_made = sem("sum_nat_made")
        sum_inverted = sem("sum_inverted")
        attn_normed = sem("attn_normed")
        attn_turned = sem("attn_turned")
        attn_styled = sem("attn_styled")
        attn_high_made = sem("attn_high_made")
        attn_low_made = sem("attn_low_made")
        o_summed = sem("o_summed")
        x1_made = sem("x1_made")
        x1m_made = sem("x1m_made")
        x1m_high_made = sem("x1m_high_made")
        x1m_low_made = sem("x1m_low_made")
        l_summed = sem("l_summed")
        y_made = sem("y_made")
        y_clipped = sem("y_clipped")
        x2_made = sem("x2_made")
        x2_turned = sem("x2_turned")
        x_out_made = sem("x_out_made")
        out_stored = [sem(f"out_stored{i}") for i in range(2)]

        def over_n(ap, groups):
            return ap.unsqueeze(2).to_broadcast([P, groups, N])

        def batches(t):
            return bass.ds(GB * t, GB) if not isinstance(t, int) else slice(GB * t, GB * t + GB)

        def column(n):
            return bass.ds(n, 1) if not isinstance(n, int) else slice(n, n + 1)

        def wait(eng, semaphore, value):
            if not isinstance(value, int) or value > 0:
                eng.wait_ge(semaphore, value)

        def whole_run(iteration):
            iteration(0, 0)
            iteration(1, 1)

            def loop(eng):
                with eng.Fori(1, G // 2 - 1) as pair:
                    iteration(pair * 2, 0)
                    iteration(pair * 2 + 1, 1)
            return loop

        def parts(t):
            if not isinstance(t, int):
                return True, True, True, True
            return t < G, t + 1 < G, 1 <= t <= G, 2 <= t <= G + 1

        def flat(tile):
            dims = " ".join("abc"[:len(tile.shape) - 1])
            return tile[:] if len(tile.shape) == 2 else tile[:].rearrange(f"p {dims} -> p ({dims})")

        aff_nat = [flat(a).rearrange("p (c s) -> p c s", c=C) for a in (xm, x1m, y)]
        w_nat = [flat(a).rearrange("p (c f) -> p c f", c=C) for a in (probs, x1, keys_strip)]
        w_sq = [flat(a).rearrange("p (c f) -> p c f", c=C) for a in (x_res[0], x_res[1], keys)]
        aff_t = flat(x_out).rearrange("p (s f) -> p s f", s=SC)
        cond_nat = flat(sum_nat)[:, 0:S]
        bias_rows = flat(sum_nat)[0:6 * C, S:S + P]
        cond_t = flat(attn_nat)[:, 0:SC * B].rearrange("p (s b) -> p s b", s=SC)
        style_sq = attn[:]
        root = keys_item[:]
        newton = sum_nat[:].rearrange("p h d -> p (h d)").rearrange("p (c b) -> p c b", c=C)

        block = ctx.enter_context(nc.Block())

        @block.sync
        def _(sp):
            sp.dma_start(cond_nat, cond).then_inc(small_loaded, 16)
            for i, vec in enumerate((k_aff_b, o_aff_b, l_aff_b, k_b, o_b, l_b)):
                sp.dma_start(bias_rows[C * i:C * (i + 1), :], vec.rearrange("(c p) -> c p", p=P))\
                  .then_inc(small_loaded, 16)
            for m, (aff, w) in enumerate(((k_aff_w, k_w), (o_aff_w, o_w), (l_aff_w, l_w))):
                sp.dma_start(aff_nat[m], aff.rearrange("(c p) s -> p c s", p=P)).then_inc(aff_loaded[m], 16)
                sp.dma_start(w_nat[m], w.rearrange("(c p) f -> p c f", p=P)).then_inc(w_loaded[m], 16)

            def load_x(t):
                wait(sp, x_turned, C * t)
                sp.dma_start(x_in[:], x[batches(t)].rearrange("b n f -> n b f")).then_inc(x_loaded, 16)

            def store_out(t, b):
                sp.wait_ge(x_out_made, GB * t + b + 1)
                sp.dma_start(out[column(GB * t + b)].rearrange("o n f -> n (o f)"), x_out[:, b % 2, :])\
                  .then_inc(out_stored[b % 2], 16)

            load_x(0)

            def iteration(t, p):
                attends, first, _, way_out = parts(t)
                if first and isinstance(t, int) and t == 0:
                    load_x(1)
                for b in range(GB):
                    if attends:
                        sp.wait_ge(max_turned, GB * t + b + 1)
                        wait(sp, shifted[U - 1], GB * t + b)
                        for q in range(P // 32):
                            sp.dma_start(max_rows[0:2, :, 32 * q:32 * q + 32].bitcast(F32),
                                         max_blocks[32 * q:32 * q + 32, :])\
                              .then_inc(max_rows_loaded, 16)
                    if b == 0 and way_out:
                        for i in range(GB):
                            store_out(t - 2, i)
                    if b == 1 and (not isinstance(t, int) or t + 2 < G):
                        load_x(t + 2)

            loop = whole_run(iteration)
            loop(sp)
            for t in range(G - 2, G + 2):
                iteration(t, t % 2)
            for i in range(2):
                sp.wait_ge(out_stored[i], 16 * (B // 2))

        @block.gpsimd
        def _(pool):
            nc.gpsimd.memset(ident[:], 0.0).then_inc(const_step, 1)
            pool.wait_ge(const_step, 1)
            nc.gpsimd.affine_select(out=ident[:], in_=ident[:], compare_op=ALU.not_equal, fill=1.0, base=0,
                                    pattern=[[-1, P]], channel_multiplier=1).then_inc(const_step, 1)
            for mask, first, value in ((same_lhs, 0.0, 1.0), (same_rhs, MASKED, 0.0)):
                nc.gpsimd.memset(mask[:], first).then_inc(const_step, 1)
                pool.wait_ge(const_step, 3 if mask is same_lhs else 5)
                nc.gpsimd.affine_select(out=mask[:], in_=mask[:], compare_op=ALU.not_equal, fill=value, base=0,
                                        pattern=[[0, mask.shape[1]], [-1, TOK], [0, H]],
                                        channel_multiplier=1).then_inc(const_step, 1)
            pool.wait_ge(mods_ready, 3)

            def x_low(t, c):
                pool.wait_ge(xm_high_made, C * t + c + 1)
                wait(pool, keys_summed, C * t)
                nc.gpsimd.tensor_tensor(xm_low[:, c, :], xm[:, c % 2, :], xm_high[:, c, :],
                                        ALU.subtract).then_inc(xm_low_made, 1)

            def attn_norm(t, b):
                pool.wait_ge(sum_inverted, GB * t + b + 1)
                nc.gpsimd.tensor_tensor(attn_nat[:], attn_nat[:], sum_inv[:].unsqueeze(2).to_broadcast([P, H, HD]),
                                        ALU.mult).then_inc(attn_normed, 1)

            def attn_split(t, b):
                pool.wait_ge(attn_high_made, GB * t + b + 1)
                wait(pool, o_summed, C * t)
                nc.gpsimd.tensor_tensor(attn_low[:, :, b, :], attn[:], attn_high[:, :, b, :],
                                        ALU.subtract).then_inc(attn_low_made, 1)

            def x1_style(t, c):
                pool.wait_ge(x1_made, C * t + c + 1)
                wait(pool, x1m_low_made, C * t + c - 1)
                nc.gpsimd.tensor_tensor(x1m[:, c % 2, :].rearrange("p (b n) -> p b n", b=GB), x1[:, c],
                                        over_n(mods[:, L_STYLE, c, batches(t)], GB),
                                        ALU.mult).then_inc(x1m_made, 1)

            def x1_low(t, c):
                pool.wait_ge(x1m_high_made, C * t + c + 1)
                nc.gpsimd.tensor_tensor(x1m_low[:, c, :], x1m[:, c % 2, :], x1m_high[:, c, :],
                                        ALU.subtract).then_inc(x1m_low_made, 1)

            def x2_add(t, c):
                pool.wait_ge(y_clipped, C * t + c + 1)
                nc.gpsimd.tensor_tensor(x1[:, c], y[:, c % 2], x1[:, c], ALU.add).then_inc(x2_made, 1)

            for c in range(C):
                x_low(0, c)

            def iteration(t, p):
                attends, first, last, way_out = parts(t)
                for b in range(GB):
                    n_t, n_b = (t - 1, GB - 1) if b == 0 else (t, b - 1)
                    before = last if b == 0 else attends
                    if before:
                        attn_norm(n_t, n_b)
                    if b == 0 and way_out:
                        x2_add(t - 2, 3)
                    if before:
                        attn_split(n_t, n_b)
                    if last and b < 2:
                        for c in (2 * b, 2 * b + 1):
                            x1_style(t - 1, c)
                            x1_low(t - 1, c)
                    if first and b == 1:
                        for c in range(C):
                            x_low(t + 1, c)
                    if last and b > 0:
                        x2_add(t - 1, b - 1)

            loop = whole_run(iteration)
            loop(pool)
            for t in range(G - 2, G + 2):
                iteration(t, t % 2)

        @block.scalar
        def _(act):
            for m in range(3):
                act.wait_ge(small_kept, 3)
                act.wait_ge(style_summed, m + 1)
                for c in range(C):
                    ins = nc.scalar.activation(mods[:, K_STYLE + m, c, :], ps_attn[:, c, :], ACT.Identity,
                                               bias=bias[:, m, c:c + 1], scale=GAIN if m == L_MAT else 1.0)
                ins.then_inc(style_made, 1)
                for i in range(C):
                    act.wait_ge(w_turned, C * m + i + 1)
                    nc.scalar.activation(w_sq[m][:, i, :], ps_scores[:, i, :], ACT.Square).then_inc(w_squared, 1)
                    nc.scalar.activation(w_high[m][:, i, :], ps_scores[:, i, :], ACT.Copy)\
                      .then_inc(w_high_made, 1)
            for m in range(3):
                act.wait_ge(norm_kept, m + 1)
                wait(act, mods_ready, m)
                nc.scalar.activation(root, mods[:, K_DEMOD + m], ACT.Sqrt).then_inc(root_made, 1)

            act.wait_ge(mods_ready, 3)

            def x_keep(t, c, p):
                act.wait_ge(xm_made, C * t + c + 1)
                wait(act, x1_made, C * (t - 2) + c + 1 if not isinstance(t, int) or t >= 2 else 0)
                ins = nc.scalar.activation(x_res[p][:, c].rearrange("p b n -> p (b n)"), ps_gen[BANK_X[c]][:],
                                           ACT.Identity, bias=bias[:, 3 + O_MAT, c:c + 1])
                ins.then_inc(x_res_made, 1)
                wait(act, keys_summed, C * t)
                nc.scalar.activation(xm_high[:, c, :], xm[:, c % 2, :], ACT.Copy).then_inc(xm_high_made, 1)

            def keys_keep(t, c):
                act.wait_ge(keys_summed, C * t + c + 1)
                wait(act, keys_turned, GB * t)
                for b in range(GB):
                    ins = nc.scalar.activation(keys[:, c, b, :], ps_gen[BANK_K[c]][:, N * b:N * (b + 1)],
                                               ACT.Identity, bias=bias[:, 3 + K_MAT, c:c + 1],
                                               scale=mods[:, K_DEMOD, c, column(GB * t + b)])
                ins.then_inc(keys_made, 1)

            def items_keep(t, b):
                act.wait_ge(items_turned, GB * t + b + 1)
                wait(act, attn_summed, GB * t + b)
                nc.scalar.activation(flat(keys_item), ps_gen[BANK_ITEMS[b]][:], ACT.Copy)\
                  .then_inc(keys_item_made, 1)

            def exp(t, b, u):
                act.wait_ge(shifted[u], GB * t + b + 1)
                wait(act, attn_summed, GB * t + b)
                nc.scalar.activation(probs[:, 2 * u:2 * u + 2].rearrange("p s q h -> p (s q h)"),
                                     ps_scores[:, 2 * u:2 * u + 2, :].rearrange("p k n -> p (k n)"),
                                     ACT.Exp, scale=SCALE).then_inc(probs_made[u], 1)

            def attn_round(t, b):
                act.wait_ge(attn_styled, GB * t + b + 1)
                wait(act, o_summed, C * t)
                nc.scalar.activation(attn_high[:, :, b, :], attn[:], ACT.Copy).then_inc(attn_high_made, 1)

            def x1_round(t, c):
                act.wait_ge(x1m_made, C * t + c + 1)
                wait(act, l_summed, C * t)
                nc.scalar.activation(x1m_high[:, c, :], x1m[:, c % 2, :], ACT.Copy).then_inc(x1m_high_made, 1)

            def y_scale(t, c):
                act.wait_ge(l_summed, C * t + c + 1)
                wait(act, x2_made, C * t + c - 1)
                for b in range(GB):
                    ins = nc.scalar.activation(y[:, c % 2, b, :], ps_gen[BANK_L[c]][:, N * b:N * (b + 1)],
                                               ACT.Identity, bias=bias[:, 3 + L_MAT, c:c + 1],
                                               scale=mods[:, L_DEMOD, c, column(GB * t + b)])
                ins.then_inc(y_made, 1)

            def out_keep(t, b):
                act.wait_ge(x2_turned, GB * t + b + 1)
                wait(act, out_stored[b % 2], 16 * (GB // 2 * t + b // 2))
                ins = nc.scalar.activation(x_out[:, b % 2, :], ps_gen[BANK_OUT[b]][:], ACT.Copy)
                ins.then_inc(x_out_made, 1)

            for c in range(C):
                x_keep(0, c, 0)
            for c in range(C):
                keys_keep(0, c)

            def iteration(t, p):
                attends, first, last, way_out = parts(t)
                for b in range(GB):
                    if b == 0 and way_out:
                        y_scale(t - 2, 3)
                    if b == 2 and last:
                        y_scale(t - 1, 1)
                    if b == 2 and first:
                        keys_keep(t + 1, 0)
                    if (last if b == 0 else attends):
                        attn_round(*((t - 1, GB - 1) if b == 0 else (t, b - 1)))
                    if b == 3 and first:
                        keys_keep(t + 1, 2)
                    if attends:
                        exp(t, b, 0)
                        exp(t, b, 1)
                    if b == 3 and first:
                        keys_keep(t + 1, 3)
                    if attends:
                        items_keep(t, b)
                    if b == 0 and way_out:
                        for i in range(GB):
                            out_keep(t - 2, i)
                    if last and b < 2:
                        x1_round(t - 1, 2 * b)
                        x1_round(t - 1, 2 * b + 1)
                    if b == 1 and first:
                        for c in range(C):
                            x_keep(t + 1, c, 1 - p)
                    if b == 1 and last:
                        y_scale(t - 1, 0)
                    if b == 2 and first:
                        keys_keep(t + 1, 1)
                    if b == 3 and last:
                        y_scale(t - 1, 2)

            loop = whole_run(iteration)
            loop(act)
            for t in range(G - 2, G + 2):
                iteration(t, t % 2)

        @block.vector
        def _(dve):
            nc.vector.memset(ones[:], 1.0).then_inc(ones_made, 1)
            dve.wait_ge(ones_made, 1)
            dve.wait_ge(const_step, 2)
            nc.vector.tensor_scalar(ones_r[:], ident[0:2, :], 0.0, 1.0, ALU.mult, ALU.add)\
              .then_inc(ones_made, 1)
            dve.wait_ge(small_turned, 1)
            nc.vector.tensor_copy(cond_t, ps_sum[:, 0:SC, :]).then_inc(small_kept, 1)
            dve.wait_ge(small_turned, 2)
            nc.vector.tensor_copy(flat(bias), ps_attn[:, 0, 0:6 * C])\
              .then_inc(small_kept, 2)
            for m in range(3):
                for s in range(SC):
                    dve.wait_ge(aff_turned, SC * m + s + 1)
                    wait(dve, style_summed, m)
                    nc.vector.tensor_copy(aff_t[:, s, :], ps_gen[s][:]).then_inc(aff_kept, 1)
                dve.wait_ge(style_made, m + 1)
                wait(dve, norm_summed, m)
                nc.vector.tensor_tensor(style_sq, mods[:, K_STYLE + m], mods[:, K_STYLE + m], ALU.mult)\
                  .then_inc(style_squared, 1)
                for i in range(C):
                    dve.wait_ge(w_high_made, C * m + i + 1)
                    nc.vector.tensor_tensor(w_low[m][:, i, :], ps_scores[:, i, :], w_high[m][:, i, :],
                                            ALU.subtract).then_inc(w_low_made, 1)
                dve.wait_ge(norm_summed, m + 1)
                nc.vector.tensor_scalar(mods[:, K_DEMOD + m], ps_sum[:], EPS, None, ALU.add).then_inc(norm_kept, 1)
            for m in range(3):
                norm = mods[:, K_DEMOD + m]
                dve.wait_ge(root_made, m + 1)
                nc.vector.reciprocal(root, root).then_inc(norm_step, 1)
                dve.wait_ge(norm_step, 4 * m + 1)
                nc.vector.tensor_tensor(newton, root, root, ALU.mult).then_inc(norm_step, 1)
                dve.wait_ge(norm_step, 4 * m + 2)
                nc.vector.tensor_tensor(newton, newton, norm, ALU.mult).then_inc(norm_step, 1)
                dve.wait_ge(norm_step, 4 * m + 3)
                nc.vector.tensor_scalar(newton, newton, -0.5, 1.5, ALU.mult, ALU.add).then_inc(norm_step, 1)
                dve.wait_ge(norm_step, 4 * m + 4)
                nc.vector.tensor_tensor(norm, newton, root, ALU.mult).then_inc(mods_ready, 1)

            def x_style(t, c):
                dve.wait_ge(x_turned, C * t + c + 1)
                wait(dve, xm_low_made, C * t + c - 1)
                nc.vector.tensor_tensor(xm[:, c % 2, :].rearrange("p (b n) -> p b n", b=GB),
                                        ps_gen[BANK_X[c]][:].rearrange("p (b n) -> p b n", b=GB),
                                        over_n(mods[:, K_STYLE, c, batches(t)], GB),
                                        ALU.mult).then_inc(xm_made, 1)

            def half_max(t, b, u):
                dve.wait_ge(scores_ready[u], GB * t + b + 1)
                nc.vector.tensor_reduce(row_max[:, 8 * u:8 * u + 8],
                                        ps_scores[:, 2 * u:2 * u + 2, :].rearrange("p s (q h) -> p s q h", q=Q),
                                        AX_X, ALU.max).then_inc(half_max_made, 1)

            def split_max(t, b):
                n = GB * t + b
                dve.wait_ge(half_max_made, 2 * n + 2)
                nc.vector.tensor_scalar(max_parts[:, 0:16], row_max[:], -1.0, None, ALU.mult)\
                  .then_inc(max_high_made, 1)
                dve.wait_ge(max_high_made, n + 1)
                nc.vector.scalar_tensor_tensor(out=max_parts[:, 16:32], in0=row_max[:], scalar=-1.0,
                                               in1=max_parts[:, 0:16], op0=ALU.mult, op1=ALU.subtract)\
                  .then_inc(max_parts_made, 1)
                dve.wait_ge(max_parts_made, n + 1)
                wait(dve, max_rows_loaded, 64 * n)
                nc.vector.transpose(max_blocks[:], max_parts[:].bitcast(F32)).then_inc(max_turned, 1)

            def keys_block(t, b):
                dve.wait_ge(keys_turned, GB * t + b + 1)
                wait(dve, items_turned, GB * (t - 1) + b + 1 if not isinstance(t, int) or t > 0 else 0)
                nc.vector.transpose(keys_strip[:, b].rearrange("p n h -> p h n"),
                                    ps_gen[BANK_KN[b]][:].rearrange("p (h d) -> p h d", h=H))\
                  .then_inc(keys_strip_made, 1)

            def attn_block(t, b):
                n = GB * t + b
                dve.wait_ge(attn_summed, n + 1)
                wait(dve, attn_turned, n)
                nc.vector.transpose(attn_nat[:], ps_attn[:].rearrange("p q (n h) -> p h (q n)", h=H))\
                  .then_inc(attn_nat_made, 1)
                nc.vector.transpose(sum_nat[:], ps_sum[:].rearrange("p q (n h) -> p h (q n)", h=H))\
                  .then_inc(sum_nat_made, 1)
                dve.wait_ge(sum_nat_made, n + 1)
                nc.vector.reciprocal(sum_inv[:], sum_nat[:, :, 0]).then_inc(sum_inverted, 1)

            def attn_style(t, b):
                dve.wait_ge(attn_turned, GB * t + b + 1)
                wait(dve, attn_low_made, GB * t + b)
                nc.vector.tensor_tensor(
                    attn[:], ps_gen[BANK_ATTN[b]][:].rearrange("p (c n) -> p c n", c=C),
                    mods[:, O_STYLE, :, column(GB * t + b)].to_broadcast([P, C, N]),
                    ALU.mult).then_inc(attn_styled, 1)

            def x1_add(t, c, p):
                dve.wait_ge(o_summed, C * t + c + 1)
                dve.wait_ge(x_res_made, C * t + c + 1)
                wait(dve, x2_turned, GB * t)
                for b in range(GB):
                    ins = nc.vector.scalar_tensor_tensor(
                        out=x1[:, c, b, :], in0=ps_gen[BANK_O[c]][:, N * b:N * (b + 1)],
                        scalar=mods[:, O_DEMOD, c, column(GB * t + b)], in1=x_res[p][:, c, b, :],
                        op0=ALU.mult, op1=ALU.add)
                ins.then_inc(x1_made, 1)

            def y_clip(t, c):
                dve.wait_ge(y_made, C * t + c + 1)
                nc.vector.tensor_scalar(y[:, c % 2], y[:, c % 2], CLAMP, -CLAMP, ALU.min, ALU.max)\
                  .then_inc(y_clipped, 1)

            for c in range(C):
                x_style(0, c)
            keys_block(0, 0)

            def iteration(t, p):
                attends, first, last, way_out = parts(t)
                for b in range(GB):
                    n_t, n_b = (t - 1, GB - 1) if b == 0 else (t, b - 1)
                    before = last if b == 0 else attends
                    if before:
                        attn_block(n_t, n_b)
                    if attends:
                        half_max(t, b, 0)
                        half_max(t, b, 1)
                        split_max(t, b)
                    if before:
                        attn_style(n_t, n_b)
                    if b == 0 and attends:
                        for i in range(1, GB):
                            keys_block(t, i)
                    if b == 0 and way_out:
                        y_clip(t - 2, 3)
                    if last and b < 2:
                        x1_add(t - 1, 2 * b, 1 - p)
                        x1_add(t - 1, 2 * b + 1, 1 - p)
                    if first and b == 1:
                        for c in range(C):
                            x_style(t + 1, c)
                    if last and b > 0:
                        y_clip(t - 1, b - 1)
                    if first and b == GB - 1:
                        keys_block(t + 1, 0)

            loop = whole_run(iteration)
            loop(dve)
            for t in range(G - 2, G + 2):
                iteration(t, t % 2)

        @block.tensor
        def _(pe):
            pe.wait_ge(const_step, 6)
            pe.wait_ge(small_loaded, 16 * 7)
            for s in range(SC):
                ins = nc.tensor.transpose(ps_sum[:, s, :], cond_nat[:, P * s:P * (s + 1)], ident[:])
            ins.then_inc(small_turned, 1)
            nc.tensor.transpose(ps_attn[:, 0, 0:6 * C], bias_rows, ident[0:6 * C, 0:6 * C])\
              .then_inc(small_turned, 1)
            for m in range(3):
                pe.wait_ge(aff_loaded[m], 16)
                for s in range(SC):
                    wait(pe, aff_kept, SC * (m - 1) + s + 1 if m else 0)
                    for c in range(C):
                        ins = nc.tensor.transpose(ps_gen[s][:, P * c:P * (c + 1)],
                                                  aff_nat[m][:, c, P * s:P * (s + 1)], ident[:])
                    ins.then_inc(aff_turned, 1)
                pe.wait_ge(aff_kept, SC * (m + 1))
                pe.wait_ge(small_kept, 3)
                wait(pe, style_made, m)
                for c in range(C):
                    for s in range(SC):
                        ins = nc.tensor.matmul(ps_attn[:, c, :], aff_t[:, s, P * c:P * (c + 1)], cond_t[:, s, :],
                                               start=(s == 0), stop=(s == SC - 1))
                ins.then_inc(style_summed, 1)
                pe.wait_ge(w_loaded[m], 16)
                for i in range(C):
                    wait(pe, w_low_made, C * (m - 1) + i + 1 if m else 0)
                    for o in range(C):
                        ins = nc.tensor.transpose(ps_scores[:, i, P * o:P * (o + 1)],
                                                  w_nat[m][:, o, P * i:P * (i + 1)], ident[:])
                    ins.then_inc(w_turned, 1)
                pe.wait_ge(w_squared, C * (m + 1))
                pe.wait_ge(style_squared, m + 1)
                wait(pe, norm_kept, m)
                for o in range(C):
                    for i in range(C):
                        ins = nc.tensor.matmul(ps_sum[:, o, :], w_sq[m][:, i, P * o:P * (o + 1)],
                                               style_sq[:, i, :], start=(i == 0), stop=(i == C - 1))
                ins.then_inc(norm_summed, 1)
            pe.wait_ge(w_low_made, 3 * C)
            pe.wait_ge(mods_ready, 3)
            pe.wait_ge(ones_made, 2)

            drained = [None, None]

            def take(bank, reader, count):
                if drained[bank]:
                    pe.wait_ge(*drained[bank])
                drained[bank] = (reader, count)
                return ps_gen[bank]

            def x_turn(t, c):
                if c == 0:
                    pe.wait_ge(x_loaded, 16 * t + 16)
                ps = take(BANK_X[c], x_res_made, C * t + c + 1)
                for b in range(GB):
                    ins = nc.tensor.transpose(ps[:, N * b:N * (b + 1)], x_in[:, b, P * c:P * (c + 1)], ident[:])
                ins.then_inc(x_turned, 1)

            def project(ps, m, c, high, low, part_ready=None):
                for i in range(C):
                    if part_ready:
                        pe.wait_ge(part_ready[0], part_ready[1] + i + 1)
                    for k, (w, a) in enumerate(((w_high[m], high), (w_low[m], high), (w_high[m], low))):
                        ins = nc.tensor.matmul(ps[:], w[:, i, P * c:P * (c + 1)], a(i),
                                               start=(i == 0 and k == 0), stop=(i == C - 1 and k == 2))
                return ins

            def k_project(t, c):
                project(take(BANK_K[c], keys_made, C * t + c + 1), K_MAT, c, lambda i: xm_high[:, i, :],
                        lambda i: xm_low[:, i, :], (xm_low_made, C * t) if c == 0 else None)\
                    .then_inc(keys_summed, 1)

            def keys_turn(t, b):
                pe.wait_ge(keys_made, C * t + C)
                ps = take(BANK_KN[b], keys_strip_made, GB * t + b + 1)
                for c in range(C):
                    ins = nc.tensor.transpose(ps[:, P * c:P * (c + 1)], keys[:, c, b, :], ident[:])
                ins.then_inc(keys_turned, 1)

            def tile_items(b, q, rows):
                return keys_strip[rows, b, TOK * q:TOK * (q + 1), :].rearrange("p n h -> p (n h)")

            def scores(t, b, u):
                pe.wait_ge(keys_strip_made, GB * t + b + 1)
                wait(pe, probs_made[u], GB * t + b)
                for s in (2 * u, 2 * u + 1):
                    nc.tensor.matmul(ps_scores[:, s, :], flat(same_lhs), flat(same_rhs),
                                     start=True, stop=False, skip_group_check=True)
                for q in range(Q):
                    for s in (2 * u, 2 * u + 1):
                        items = tile_items(b, q, slice(32 * s, 32 * s + 32))
                        ins = nc.tensor.matmul(ps_scores[:, s, P * q:P * (q + 1)], items, items,
                                               start=False, stop=False, skip_group_check=True)
                ins.then_inc(scores_ready[u], 1)

            def items_turn(t, b):
                ps = take(BANK_ITEMS[b], keys_item_made, GB * t + b + 1)
                for q in range(Q):
                    ins = nc.tensor.transpose(ps[:, P * q:P * (q + 1)], tile_items(b, q, slice(0, P)), ident[:])
                ins.then_inc(items_turned, 1)

            def shift(t, b, u):
                pe.wait_ge(max_rows_loaded, 64 * (GB * t + b) + 64)
                for i in (2 * u, 2 * u + 1):
                    ins = nc.tensor.matmul(
                        ps_scores[:, i, :], ones_r[:],
                        max_rows[:, Q * i:Q * (i + 1), :].rearrange("s q h -> s (q h)"),
                        start=False, stop=True, skip_group_check=True)
                ins.then_inc(shifted[u], 1)

            def attend(t, b):
                n = GB * t + b
                pe.wait_ge(keys_item_made, n + 1)
                for u in range(U):
                    pe.wait_ge(probs_made[u], n + 1)
                wait(pe, sum_nat_made, n)
                for q in range(Q):
                    for ps in (ps_attn, ps_sum):
                        for s in range(ROWS):
                            strip = slice(32 * s, 32 * s + 32)
                            ins = nc.tensor.matmul(ps[strip, q, :],
                                                   ones[:] if ps is ps_sum else keys_item[:, q, strip],
                                                   probs[:, s, q, :], start=True, stop=True)
                ins.then_inc(attn_summed, 1)

            def attn_turn(t, b):
                pe.wait_ge(attn_normed, GB * t + b + 1)
                ps = take(BANK_ATTN[b], attn_styled, GB * t + b + 1)
                for c in range(C):
                    ins = nc.tensor.transpose(ps[:, P * c:P * (c + 1)], flat(attn_nat)[:, P * c:P * (c + 1)],
                                              ident[:])
                ins.then_inc(attn_turned, 1)

            def o_project(t, c):
                if c == 0:
                    pe.wait_ge(attn_low_made, GB * t + GB)
                project(take(BANK_O[c], x1_made, C * t + c + 1), O_MAT, c,
                        lambda i: attn_high[:, i].rearrange("p b n -> p (b n)"),
                        lambda i: attn_low[:, i].rearrange("p b n -> p (b n)")).then_inc(o_summed, 1)

            def l_project(t, c):
                project(take(BANK_L[c], y_made, C * t + c + 1), L_MAT, c, lambda i: x1m_high[:, i, :],
                        lambda i: x1m_low[:, i, :], (x1m_low_made, C * t) if c == 0 else None)\
                    .then_inc(l_summed, 1)

            def x2_turn(t, b):
                if b == 0:
                    pe.wait_ge(x2_made, C * t + C)
                ps = take(BANK_OUT[b], x_out_made, GB * t + b + 1)
                for c in range(C):
                    ins = nc.tensor.transpose(ps[:, P * c:P * (c + 1)], x1[:, c, b, :], ident[:])
                ins.then_inc(x2_turned, 1)

            for c in range(C):
                x_turn(0, c)
            for c in range(C):
                k_project(0, c)
            keys_turn(0, 0)

            def iteration(t, p):
                attends, first, last, way_out = parts(t)
                if not isinstance(t, int) and p == 0:
                    drained[BANK_L[2]] = (y_made, C * (t - 2) + 3)
                    drained[BANK_KN[0]] = (keys_strip_made, GB * t + 1)
                for b in range(GB):
                    if attends:
                        scores(t, b, 0)
                        scores(t, b, 1)
                    if (last if b == 0 else attends):
                        attn_turn(*((t - 1, GB - 1) if b == 0 else (t, b - 1)))
                    if b == 0 and way_out:
                        l_project(t - 2, 3)
                    if b == 0 and attends:
                        for i in range(1, GB):
                            keys_turn(t, i)
                    if b == 1 and last:
                        o_project(t - 1, 2)
                        o_project(t - 1, 3)
                    if b == 2 and last:
                        l_project(t - 1, 1)
                    if b == 2 and first:
                        k_project(t + 1, 0)
                    if b == 3 and first:
                        k_project(t + 1, 2)
                        k_project(t + 1, 3)
                    if attends:
                        shift(t, b, 0)
                        shift(t, b, 1)
                        items_turn(t, b)
                    if b == 0 and way_out:
                        for i in range(GB):
                            x2_turn(t - 2, i)
                    if b == 0 and last:
                        o_project(t - 1, 0)
                        o_project(t - 1, 1)
                    if b == 1 and first:
                        for c in range(C):
                            x_turn(t + 1, c)
                    if b == 1 and last:
                        l_project(t - 1, 0)
                    if b == 2 and first:
                        k_project(t + 1, 1)
                    if b == 3 and last:
                        l_project(t - 1, 2)
                    if b == 3 and first:
                        keys_turn(t + 1, 0)
                    if attends:
                        attend(t, b)

            loop = whole_run(iteration)
            loop(pe)
            drained[BANK_L[2]] = (y_made, C * (G - 4) + 3)
            drained[BANK_KN[0]] = (keys_strip_made, GB * (G - 2) + 1)
            for t in range(G - 2, G + 2):
                iteration(t, t % 2)


_INS = ["x", "cond_512", "L0_cond_k_aff_w", "L0_cond_k_aff_b", "L0_cond_k_w", "L0_cond_k_b",
        "L0_cond_o_aff_w", "L0_cond_o_aff_b", "L0_cond_o_w", "L0_cond_o_b",
        "L1_cond_weight", "L1_cond_bias", "L1_cond_affine_w", "L1_cond_affine_b"]


def kernel(**inputs):
    import numpy as _np
    import concourse.bacc as _bacc
    from concourse.bass_utils import run_bass_kernel_spmd as _run

    nc = _bacc.Bacc("TRN2", target_bir_lowering=False, num_devices=1)
    arrays, args = {}, []
    for name in _INS:
        a = _np.ascontiguousarray(inputs[name])
        arrays[f"in_{name}_dram"] = a
        args.append(nc.dram_tensor(f"in_{name}_dram", a.shape, mybir.dt.from_np(a.dtype), kind="ExternalInput").ap())
    shape = inputs["x"].shape
    args.append(nc.dram_tensor("out_dram", shape, F32, kind="ExternalOutput").ap())
    modulated_chain_kernel(nc, *args)
    r = _run(nc, [arrays], core_ids=[0])
    return r.results[0]["out_dram"]
```

```python
from contextlib import ExitStack

import concourse.bass as bass
from concourse import mybir

F32 = mybir.dt.float32
F32R = mybir.dt.float32r
BF16 = mybir.dt.bfloat16
ALU = mybir.AluOpType
ACT = mybir.ActivationFunctionType
AX_X = mybir.AxisListType.X

P = 128
HD = 32
EPS = 1e-8
CLAMP = 256.0
MASKED = -1e30

K_STYLE, O_STYLE, L_STYLE, K_DEMOD, O_DEMOD, L_DEMOD = range(6)
K_MAT, O_MAT, L_MAT = range(3)

BANK_K = (1, 2, 0, 1)
BANK_O = (2, 0, 1, 2)
BANK_L = (2, 0, 1, 0)
BANK_KN = (3, 3, 5, 3)
BANK_ITEMS = (4, 5, 3, 5)
BANK_ATTN = (4, 4, 4, 4)
BANK_OUT = (3, 4, 5, 3)
BANK_X = (5, 3, 4, 0)


def modulated_chain_kernel(nc, x, cond, k_aff_w, k_aff_b, k_w, k_b, o_aff_w, o_aff_b, o_w, o_b,
                           l_w, l_b, l_aff_w, l_aff_b, out):
    B, N, F = x.shape
    S = cond.shape[1]
    C = F // P
    GB = 512 // N
    G = B // GB
    SC = S // P
    H = F // HD
    STRIPS = P // HD
    QUADS = P // HD
    PAIR = HD // H
    Q = HD // PAIR // QUADS
    SCALE = 1.0 / float(HD) ** 0.5
    GAIN = 1.0 / float(S) ** 0.5
    assert N == P and B == P and C == 4 and GB == 4 and Q == 4 and G % 2 == 0
    assert HD == 32 and PAIR * H == HD

    with ExitStack() as ctx:
        def sb(name, shape, dt=F32):
            return ctx.enter_context(nc.sbuf_tensor(name, shape, dt))

        def sem(name):
            return ctx.enter_context(nc.semaphore(name))

        w_high = [sb(f"w_high{m}", [P, C, F], F32R) for m in range(3)]
        w_low = [sb(f"w_low{m}", [P, C, F], F32R) for m in range(3)]
        mods = sb("mods", [P, 6, C, B])
        bias = sb("bias", [P, 6, C])
        ident = sb("ident", [P, P])
        same_lhs = sb("same_lhs", [P, QUADS, PAIR, H], BF16)
        same_rhs = sb("same_rhs", [P, Q * STRIPS, PAIR, H], BF16)

        x_in = sb("x_in", [P, GB, F])
        x_res = [sb(f"x_res{p}", [P, C, GB, N]) for p in range(2)]
        xm = sb("xm", [P, 2, GB * N])
        xm_high = sb("xm_high", [P, C, GB * N], F32R)
        xm_low = sb("xm_low", [P, C, GB * N], F32R)
        keys = sb("keys", [P, C, GB, N])
        keys_strip = sb("keys_strip", [P, GB, 32, H])
        keys_spread = sb("keys_spread", [P, STRIPS, HD * H])
        keys_item = sb("keys_item", [P, Q, P])
        row_max = sb("row_max", [P, Q * STRIPS])
        row_sum = sb("row_sum", [P, Q * STRIPS])
        row_inv = sb("row_inv", [P, Q * STRIPS])
        soft = sb("soft", [P, Q * STRIPS, HD])
        probs = sb("probs", [P, Q * STRIPS, HD])
        probs_spread = sb("probs_spread", [P, QUADS, Q * STRIPS * HD])
        attn_nat = sb("attn_nat", [P, H, HD])
        attn = sb("attn", [P, C, N])
        attn_high = sb("attn_high", [P, C, GB, N], F32R)
        attn_low = sb("attn_low", [P, C, GB, N], F32R)
        x1 = sb("x1", [P, C, GB, N])
        x1m = sb("x1m", [P, 2, GB * N])
        x1m_high = sb("x1m_high", [P, C, GB * N], F32R)
        x1m_low = sb("x1m_low", [P, C, GB * N], F32R)
        y = sb("y", [P, 2, GB, N])
        x_out = sb("x_out", [P, GB, F])

        ps_scores = ctx.enter_context(nc.psum_tensor("ps_scores", [P, Q * STRIPS, HD], F32))
        ps_attn = ctx.enter_context(nc.psum_tensor("ps_attn", [P, Q, P], F32))
        ps_gen = [ctx.enter_context(nc.psum_tensor(f"ps_gen{i}", [P, 512], F32)) for i in range(6)]

        small_loaded = sem("small_loaded")
        aff_loaded = [sem(f"aff_loaded{m}") for m in range(3)]
        w_loaded = [sem(f"w_loaded{m}") for m in range(3)]
        const_step = sem("const_step")
        small_turned = sem("small_turned")
        small_kept = sem("small_kept")
        aff_turned = sem("aff_turned")
        aff_kept = sem("aff_kept")
        style_summed = sem("style_summed")
        style_made = sem("style_made")
        style_squared = sem("style_squared")
        w_turned = sem("w_turned")
        w_high_made = sem("w_high_made")
        w_low_made = sem("w_low_made")
        w_squared = sem("w_squared")
        norm_summed = sem("norm_summed")
        norm_kept = sem("norm_kept")
        norm_step = sem("norm_step")
        root_made = sem("root_made")
        mods_ready = sem("mods_ready")

        x_loaded = sem("x_loaded")
        x_turned = sem("x_turned")
        xm_made = sem("xm_made")
        x_res_made = sem("x_res_made")
        xm_high_made = sem("xm_high_made")
        xm_low_made = sem("xm_low_made")
        keys_summed = sem("keys_summed")
        keys_made = sem("keys_made")
        keys_turned = sem("keys_turned")
        keys_strip_made = sem("keys_strip_made")
        items_turned = sem("items_turned")
        keys_spread_made = sem("keys_spread_made")
        keys_item_made = sem("keys_item_made")
        scores_ready = sem("scores_ready")
        max_made = sem("max_made")
        shifted = sem("shifted")
        exp_made = sem("exp_made")
        sum_made = sem("sum_made")
        sum_inverted = sem("sum_inverted")
        soft_made = sem("soft_made")
        probs_made = sem("probs_made")
        probs_spread_made = sem("probs_spread_made")
        attn_summed = sem("attn_summed")
        attn_nat_made = sem("attn_nat_made")
        attn_turned = sem("attn_turned")
        attn_styled = sem("attn_styled")
        attn_high_made = sem("attn_high_made")
        attn_low_made = sem("attn_low_made")
        o_summed = sem("o_summed")
        x1_made = sem("x1_made")
        x1m_made = sem("x1m_made")
        x1m_high_made = sem("x1m_high_made")
        x1m_low_made = sem("x1m_low_made")
        l_summed = sem("l_summed")
        y_made = sem("y_made")
        y_clipped = sem("y_clipped")
        x2_made = sem("x2_made")
        x2_turned = sem("x2_turned")
        x_out_made = sem("x_out_made")
        out_stored = sem("out_stored")
        spread_zeroed = sem("spread_zeroed")

        def over_n(ap, groups):
            return ap.unsqueeze(2).to_broadcast([P, groups, N])

        def batches(t):
            return bass.ds(GB * t, GB) if not isinstance(t, int) else slice(GB * t, GB * t + GB)

        def column(n):
            return bass.ds(n, 1) if not isinstance(n, int) else slice(n, n + 1)

        def wait(eng, semaphore, value):
            if not isinstance(value, int) or value > 0:
                eng.wait_ge(semaphore, value)

        def whole_run(iteration):
            iteration(0, 0)
            iteration(1, 1)

            def loop(eng):
                with eng.Fori(1, G // 2 - 1) as pair:
                    iteration(pair * 2, 0)
                    iteration(pair * 2 + 1, 1)
            return loop

        def parts(t):
            if not isinstance(t, int):
                return True, True, True, True
            return t < G, t + 1 < G, 1 <= t <= G, 2 <= t <= G + 1

        def flat(tile):
            dims = " ".join("abc"[:len(tile.shape) - 1])
            return tile[:] if len(tile.shape) == 2 else tile[:].rearrange(f"p {dims} -> p ({dims})")

        aff_nat = [flat(a).rearrange("p (c s) -> p c s", c=C) for a in (xm, x1m, y)]
        w_nat = [flat(a).rearrange("p (c f) -> p c f", c=C) for a in (probs_spread, x1, keys_strip)]
        w_sq = [flat(a).rearrange("p (c f) -> p c f", c=C) for a in (x_res[0], x_res[1], keys)]
        aff_t = flat(x_out)[:, 0:SC * F].rearrange("p (s f) -> p s f", s=SC)
        cond_nat = flat(probs)[:, 0:S]
        bias_rows = flat(probs)[0:6 * C, S:S + P]
        cond_t = flat(attn_nat)[:, 0:SC * B].rearrange("p (s b) -> p s b", s=SC)
        style_sq = attn[:]
        root = keys_item[:]
        newton = flat(soft).rearrange("p (c b) -> p c b", c=C)

        ps_norm = ps_scores[:].rearrange("p k h -> p (k h)").rearrange("p (c b) -> p c b", c=C)

        block = ctx.enter_context(nc.Block())

        @block.sync
        def _(sp):
            sp.dma_start(cond_nat, cond).then_inc(small_loaded, 16)
            for i, vec in enumerate((k_aff_b, o_aff_b, l_aff_b, k_b, o_b, l_b)):
                sp.dma_start(bias_rows[C * i:C * (i + 1), :], vec.rearrange("(c p) -> c p", p=P))\
                  .then_inc(small_loaded, 16)
            for m, (aff, w) in enumerate(((k_aff_w, k_w), (o_aff_w, o_w), (l_aff_w, l_w))):
                sp.dma_start(aff_nat[m], aff.rearrange("(c p) s -> p c s", p=P)).then_inc(aff_loaded[m], 16)
                sp.dma_start(w_nat[m], w.rearrange("(c p) f -> p c f", p=P)).then_inc(w_loaded[m], 16)

            def load_x(t):
                wait(sp, x_turned, C * t)
                sp.dma_start(x_in[:], x[batches(t)].rearrange("b n f -> n b f")).then_inc(x_loaded, 16)

            def store_out(t):
                sp.wait_ge(x_out_made, GB * t + GB)
                sp.dma_start(out[batches(t)].rearrange("b n f -> n b f"), x_out[:]).then_inc(out_stored, 16)

            def spread_keys(t, b):
                n = GB * t + b
                sp.wait_ge(keys_strip_made, n + 1)
                if b != 1:
                    wait(sp, scores_ready, n)
                for s in range(STRIPS):
                    strip = slice(HD * s, HD * s + HD)
                    sp.dma_start(keys_spread[strip, s, :], keys_strip[strip, b].rearrange("p n h -> p (n h)"))\
                      .then_inc(keys_spread_made, 16)

            def spread_probs(t, b):
                n = GB * t + b
                sp.wait_ge(probs_made, n + 1)
                wait(sp, attn_summed, n)
                for s in range(QUADS):
                    quad = slice(HD * s, HD * s + HD)
                    sp.dma_start(probs_spread[quad, s, :], probs[quad].rearrange("p k h -> p (k h)"))\
                      .then_inc(probs_spread_made, 16)

            load_x(0)
            sp.wait_ge(spread_zeroed, 1)
            spread_keys(0, 0)

            def iteration(t, p):
                attends, first, _, way_out = parts(t)
                if first and isinstance(t, int) and t == 0:
                    load_x(1)
                for b in range(GB):
                    if attends and b < GB - 1:
                        spread_keys(t, b + 1)
                    if attends:
                        if isinstance(t, int) and t == 0 and b == 0:
                            sp.wait_ge(spread_zeroed, 2)
                        spread_probs(t, b)
                    if b == 1 and way_out:
                        store_out(t - 2)
                    if b == 2 and (not isinstance(t, int) or t + 2 < G):
                        load_x(t + 2)
                    if first and b == GB - 1:
                        spread_keys(t + 1, 0)

            loop = whole_run(iteration)
            loop(sp)
            for t in range(G - 2, G + 2):
                iteration(t, t % 2)
            sp.wait_ge(out_stored, 16 * G)

        @block.gpsimd
        def _(pool):
            nc.gpsimd.memset(ident[:], 0.0).then_inc(const_step, 1)
            pool.wait_ge(const_step, 1)
            nc.gpsimd.affine_select(out=ident[:], in_=ident[:], compare_op=ALU.not_equal, fill=1.0, base=0,
                                    pattern=[[-1, P]], channel_multiplier=1).then_inc(const_step, 1)
            for mask, first, value in ((same_lhs, 0.0, 1.0), (same_rhs, MASKED, 0.0)):
                nc.gpsimd.memset(mask[:], first).then_inc(const_step, 1)
                pool.wait_ge(const_step, 3 if mask is same_lhs else 5)
                nc.gpsimd.affine_select(out=mask[:], in_=mask[:], compare_op=ALU.not_equal, fill=value, base=0,
                                        pattern=[[0, mask.shape[1]], [-1, PAIR], [0, H]],
                                        channel_multiplier=1).then_inc(const_step, 1)
            nc.gpsimd.memset(keys_spread[:], 0.0).then_inc(spread_zeroed, 1)
            pool.wait_ge(mods_ready, 3)

            def x_low(t, c):
                pool.wait_ge(xm_high_made, C * t + c + 1)
                wait(pool, keys_summed, C * t)
                nc.gpsimd.tensor_tensor(xm_low[:, c, :], xm[:, c % 2, :], xm_high[:, c, :],
                                        ALU.subtract).then_inc(xm_low_made, 1)

            def normalise(t, b):
                pool.wait_ge(sum_inverted, GB * t + b + 1)
                nc.gpsimd.tensor_tensor(soft[:], soft[:], row_inv[:].unsqueeze(2).to_broadcast(soft.shape),
                                        ALU.mult).then_inc(soft_made, 1)

            def attn_split(t, b):
                pool.wait_ge(attn_high_made, GB * t + b + 1)
                wait(pool, o_summed, C * t)
                nc.gpsimd.tensor_tensor(attn_low[:, :, b, :], attn[:], attn_high[:, :, b, :],
                                        ALU.subtract).then_inc(attn_low_made, 1)

            def x1_low(t, c):
                pool.wait_ge(x1m_high_made, C * t + c + 1)
                nc.gpsimd.tensor_tensor(x1m_low[:, c, :], x1m[:, c % 2, :], x1m_high[:, c, :],
                                        ALU.subtract).then_inc(x1m_low_made, 1)

            def x2_add(t, c):
                pool.wait_ge(y_clipped, C * t + c + 1)
                nc.gpsimd.tensor_tensor(x1[:, c], y[:, c % 2], x1[:, c], ALU.add).then_inc(x2_made, 1)

            for c in range(C):
                x_low(0, c)
            nc.gpsimd.memset(probs_spread[:], 0.0).then_inc(spread_zeroed, 1)

            def iteration(t, p):
                attends, first, last, way_out = parts(t)
                for b in range(GB):
                    if b == 2 and first:
                        x_low(t + 1, 2)
                        x_low(t + 1, 3)
                    if attends:
                        normalise(t, b)
                    if b == 0 and way_out:
                        x2_add(t - 2, 1)
                    if b == 0 and last:
                        attn_split(t - 1, 3)
                    if b == 0 and way_out:
                        x2_add(t - 2, 2)
                        x2_add(t - 2, 3)
                    if b == 1 and last:
                        x1_low(t - 1, 0)
                        x1_low(t - 1, 1)
                    if b == 1 and first:
                        x_low(t + 1, 0)
                        x_low(t + 1, 1)
                    if b == 2 and attends:
                        attn_split(t, 0)
                        attn_split(t, 1)
                    if b == 2 and last:
                        x1_low(t - 1, 2)
                        x1_low(t - 1, 3)
                    if b == 3 and attends:
                        attn_split(t, 2)
                    if b == 3 and last:
                        x2_add(t - 1, 0)

            loop = whole_run(iteration)
            loop(pool)
            for t in range(G - 2, G + 2):
                iteration(t, t % 2)

        @block.scalar
        def _(act):
            for m in range(3):
                act.wait_ge(small_kept, 3)
                act.wait_ge(style_summed, m + 1)
                for c in range(C):
                    ins = nc.scalar.activation(mods[:, K_STYLE + m, c, :], ps_attn[:, c, :], ACT.Identity,
                                               bias=bias[:, m, c:c + 1], scale=GAIN if m == L_MAT else 1.0)
                ins.then_inc(style_made, 1)
                for i in range(C):
                    act.wait_ge(w_turned, C * m + i + 1)
                    nc.scalar.activation(w_sq[m][:, i, :], ps_gen[i][:], ACT.Square).then_inc(w_squared, 1)
                    nc.scalar.activation(w_high[m][:, i, :], ps_gen[i][:], ACT.Copy)\
                      .then_inc(w_high_made, 1)
            for m in range(3):
                act.wait_ge(norm_kept, m + 1)
                wait(act, mods_ready, m)
                nc.scalar.activation(root, mods[:, K_DEMOD + m], ACT.Sqrt).then_inc(root_made, 1)

            act.wait_ge(mods_ready, 3)

            def x_keep(t, c, p):
                act.wait_ge(xm_made, C * t + c + 1)
                wait(act, keys_summed, C * t)
                nc.scalar.activation(xm_high[:, c, :], xm[:, c % 2, :], ACT.Copy).then_inc(xm_high_made, 1)
                wait(act, x1_made, C * (t - 2) + c + 1 if not isinstance(t, int) or t >= 2 else 0)
                ins = nc.scalar.activation(x_res[p][:, c].rearrange("p b n -> p (b n)"), ps_gen[BANK_X[c]][:],
                                           ACT.Identity, bias=bias[:, 3 + O_MAT, c:c + 1])
                ins.then_inc(x_res_made, 1)

            def keys_keep(t, c):
                act.wait_ge(keys_summed, C * t + c + 1)
                wait(act, keys_turned, GB * t)
                for b in range(GB):
                    ins = nc.scalar.activation(keys[:, c, b, :], ps_gen[BANK_K[c]][:, N * b:N * (b + 1)],
                                               ACT.Identity, bias=bias[:, 3 + K_MAT, c:c + 1],
                                               scale=mods[:, K_DEMOD, c, column(GB * t + b)])
                ins.then_inc(keys_made, 1)

            def items_keep(t, b):
                act.wait_ge(items_turned, GB * t + b + 1)
                wait(act, attn_summed, GB * t + b)
                nc.scalar.activation(flat(keys_item), ps_gen[BANK_ITEMS[b]][:], ACT.Copy)\
                  .then_inc(keys_item_made, 1)

            def exp(t, b):
                act.wait_ge(shifted, GB * t + b + 1)
                nc.scalar.activation(soft[:], soft[:], ACT.Exp, scale=SCALE).then_inc(exp_made, 1)

            def attn_round(t, b):
                act.wait_ge(attn_styled, GB * t + b + 1)
                wait(act, o_summed, C * t)
                nc.scalar.activation(attn_high[:, :, b, :], attn[:], ACT.Copy).then_inc(attn_high_made, 1)

            def x1_round(t, c):
                act.wait_ge(x1m_made, C * t + c + 1)
                wait(act, l_summed, C * t)
                nc.scalar.activation(x1m_high[:, c, :], x1m[:, c % 2, :], ACT.Copy).then_inc(x1m_high_made, 1)

            def y_scale(t, c):
                act.wait_ge(l_summed, C * t + c + 1)
                wait(act, x2_made, C * t + c - 1)
                for b in range(GB):
                    ins = nc.scalar.activation(y[:, c % 2, b, :], ps_gen[BANK_L[c]][:, N * b:N * (b + 1)],
                                               ACT.Identity, bias=bias[:, 3 + L_MAT, c:c + 1],
                                               scale=mods[:, L_DEMOD, c, column(GB * t + b)])
                ins.then_inc(y_made, 1)

            def out_keep(t, b):
                act.wait_ge(x2_turned, GB * t + b + 1)
                if b == 0:
                    wait(act, out_stored, 16 * t)
                nc.scalar.activation(x_out[:, b, :], ps_gen[BANK_OUT[b]][:], ACT.Copy).then_inc(x_out_made, 1)

            for c in range(C):
                x_keep(0, c, 0)
            for c in range(C):
                keys_keep(0, c)

            def iteration(t, p):
                attends, first, last, way_out = parts(t)
                for b in range(GB):
                    if attends:
                        exp(t, b)
                    if b == 0 and way_out:
                        y_scale(t - 2, 2)
                    if b == 2 and first:
                        x_keep(t + 1, 3, 1 - p)
                    if b == 2 and attends:
                        attn_round(t, 0)
                    if b == 3 and first:
                        keys_keep(t + 1, 2)
                        keys_keep(t + 1, 3)
                    if attends:
                        items_keep(t, b)
                    if b == 0 and last:
                        attn_round(t - 1, 3)
                    if b == 0 and way_out:
                        y_scale(t - 2, 3)
                    if b == 1 and way_out:
                        for i in range(GB):
                            out_keep(t - 2, i)
                    if b == 1 and last:
                        x1_round(t - 1, 0)
                        x1_round(t - 1, 1)
                    if b == 1 and first:
                        x_keep(t + 1, 0, 1 - p)
                        x_keep(t + 1, 1, 1 - p)
                    if b == 1 and last:
                        x1_round(t - 1, 2)
                    if b == 1 and first:
                        x_keep(t + 1, 2, 1 - p)
                    if b == 2 and last:
                        x1_round(t - 1, 3)
                    if b == 2 and attends:
                        attn_round(t, 1)
                    if b == 2 and first:
                        keys_keep(t + 1, 0)
                        keys_keep(t + 1, 1)
                    if b == 3 and last:
                        y_scale(t - 1, 0)
                    if b == 3 and attends:
                        attn_round(t, 2)
                    if b == 3 and last:
                        y_scale(t - 1, 1)

            loop = whole_run(iteration)
            loop(act)
            for t in range(G - 2, G + 2):
                iteration(t, t % 2)

        @block.vector
        def _(dve):
            dve.wait_ge(small_turned, 1)
            nc.vector.tensor_copy(cond_t, ps_norm[:, 0:SC, :]).then_inc(small_kept, 1)
            dve.wait_ge(small_turned, 2)
            nc.vector.tensor_copy(flat(bias), ps_attn[:, 0, 0:6 * C])\
              .then_inc(small_kept, 2)
            for m in range(3):
                for s in range(SC):
                    dve.wait_ge(aff_turned, SC * m + s + 1)
                    wait(dve, style_summed, m)
                    nc.vector.tensor_copy(aff_t[:, s, :], ps_gen[4 + s][:]).then_inc(aff_kept, 1)
                dve.wait_ge(style_made, m + 1)
                wait(dve, norm_summed, m)
                nc.vector.tensor_tensor(style_sq, mods[:, K_STYLE + m], mods[:, K_STYLE + m], ALU.mult)\
                  .then_inc(style_squared, 1)
                for i in range(C):
                    dve.wait_ge(w_high_made, C * m + i + 1)
                    nc.vector.tensor_tensor(w_low[m][:, i, :], ps_gen[i][:], w_high[m][:, i, :],
                                            ALU.subtract).then_inc(w_low_made, 1)
                dve.wait_ge(norm_summed, m + 1)
                nc.vector.tensor_scalar(mods[:, K_DEMOD + m], ps_norm, EPS, None, ALU.add).then_inc(norm_kept, 1)
            for m in range(3):
                norm = mods[:, K_DEMOD + m]
                dve.wait_ge(root_made, m + 1)
                nc.vector.reciprocal(root, root).then_inc(norm_step, 1)
                dve.wait_ge(norm_step, 4 * m + 1)
                nc.vector.tensor_tensor(newton, root, root, ALU.mult).then_inc(norm_step, 1)
                dve.wait_ge(norm_step, 4 * m + 2)
                nc.vector.tensor_tensor(newton, newton, norm, ALU.mult).then_inc(norm_step, 1)
                dve.wait_ge(norm_step, 4 * m + 3)
                nc.vector.tensor_scalar(newton, newton, -0.5, 1.5, ALU.mult, ALU.add).then_inc(norm_step, 1)
                dve.wait_ge(norm_step, 4 * m + 4)
                nc.vector.tensor_tensor(norm, newton, root, ALU.mult).then_inc(mods_ready, 1)

            def x_style(t, c):
                dve.wait_ge(x_turned, C * t + c + 1)
                wait(dve, xm_low_made, C * t + c - 1)
                nc.vector.tensor_tensor(xm[:, c % 2, :].rearrange("p (b n) -> p b n", b=GB),
                                        ps_gen[BANK_X[c]][:].rearrange("p (b n) -> p b n", b=GB),
                                        over_n(mods[:, K_STYLE, c, batches(t)], GB),
                                        ALU.mult).then_inc(xm_made, 1)

            def shift(t, b):
                n = GB * t + b
                dve.wait_ge(scores_ready, n + 1)
                nc.vector.tensor_reduce(row_max[:], ps_scores[:], AX_X, ALU.max).then_inc(max_made, 1)
                dve.wait_ge(max_made, n + 1)
                nc.vector.tensor_tensor(soft[:], ps_scores[:], row_max[:].unsqueeze(2).to_broadcast(soft.shape),
                                        ALU.subtract).then_inc(shifted, 1)

            def row_sums(t, b):
                n = GB * t + b
                dve.wait_ge(exp_made, n + 1)
                nc.vector.tensor_reduce(row_sum[:], soft[:], AX_X, ALU.add).then_inc(sum_made, 1)
                dve.wait_ge(sum_made, n + 1)
                nc.vector.reciprocal(row_inv[:], row_sum[:]).then_inc(sum_inverted, 1)

            def probs_block(t, b):
                dve.wait_ge(soft_made, GB * t + b + 1)
                wait(dve, probs_spread_made, 64 * (GB * t + b))
                nc.vector.transpose(flat(probs), flat(soft)).then_inc(probs_made, 1)

            def keys_block(t, b):
                dve.wait_ge(keys_turned, GB * t + b + 1)
                wait(dve, items_turned, GB * (t - 1) + b + 1 if not isinstance(t, int) or t > 0 else 0)
                nc.vector.transpose(keys_strip[:, b].rearrange("p n h -> p h n"),
                                    ps_gen[BANK_KN[b]][:].rearrange("p (h d) -> p h d", h=H))\
                  .then_inc(keys_strip_made, 1)

            def attn_block(t, b):
                n = GB * t + b
                dve.wait_ge(attn_summed, n + 1)
                wait(dve, attn_turned, n)
                nc.vector.transpose(attn_nat[:], ps_attn[:].rearrange("p q (n h) -> p h (q n)", h=H))\
                  .then_inc(attn_nat_made, 1)

            def attn_style(t, b):
                dve.wait_ge(attn_turned, GB * t + b + 1)
                wait(dve, attn_low_made, GB * t + b)
                nc.vector.tensor_tensor(
                    attn[:], ps_gen[BANK_ATTN[b]][:].rearrange("p (c n) -> p c n", c=C),
                    mods[:, O_STYLE, :, column(GB * t + b)].to_broadcast([P, C, N]),
                    ALU.mult).then_inc(attn_styled, 1)

            def x1_add(t, c, p):
                dve.wait_ge(o_summed, C * t + c + 1)
                dve.wait_ge(x_res_made, C * t + c + 1)
                wait(dve, x2_turned, GB * t)
                for b in range(GB):
                    ins = nc.vector.scalar_tensor_tensor(
                        out=x1[:, c, b, :], in0=ps_gen[BANK_O[c]][:, N * b:N * (b + 1)],
                        scalar=mods[:, O_DEMOD, c, column(GB * t + b)], in1=x_res[p][:, c, b, :],
                        op0=ALU.mult, op1=ALU.add)
                ins.then_inc(x1_made, 1)

            def x1_style(t, c):
                dve.wait_ge(x1_made, C * t + c + 1)
                wait(dve, x1m_low_made, C * t + c - 1)
                nc.vector.tensor_tensor(x1m[:, c % 2, :].rearrange("p (b n) -> p b n", b=GB), x1[:, c],
                                        over_n(mods[:, L_STYLE, c, batches(t)], GB),
                                        ALU.mult).then_inc(x1m_made, 1)

            def y_clip(t, c):
                dve.wait_ge(y_made, C * t + c + 1)
                nc.vector.tensor_scalar(y[:, c % 2], y[:, c % 2], CLAMP, -CLAMP, ALU.min, ALU.max)\
                  .then_inc(y_clipped, 1)

            for c in range(C):
                x_style(0, c)
            keys_block(0, 0)

            def iteration(t, p):
                attends, first, last, way_out = parts(t)

                def x1_make(c):
                    x1_add(t - 1, c, 1 - p)
                    x1_style(t - 1, c)

                for b in range(GB):
                    n_t, n_b = (t - 1, GB - 1) if b == 0 else (t, b - 1)
                    before = last if b == 0 else attends
                    if attends:
                        shift(t, b)
                    if b == 0 and attends:
                        keys_block(t, 1)
                    if b == 2 and first:
                        x_style(t + 1, 3)
                    if attends:
                        row_sums(t, b)
                    if b == 2 and last:
                        x1_add(t - 1, 3, 1 - p)
                    if b == 0 and way_out:
                        y_clip(t - 2, 1)
                    if attends and b == 3:
                        probs_block(t, b)
                    if before:
                        attn_block(n_t, n_b)
                    if attends and b < 3:
                        probs_block(t, b)
                    if b == 0 and attends:
                        keys_block(t, 2)
                        keys_block(t, 3)
                    if b == 1 and last:
                        x1_make(0)
                    if b == 2 and last:
                        x1_style(t - 1, 3)
                    if b == 3 and first:
                        keys_block(t + 1, 0)
                    if before:
                        attn_style(n_t, n_b)
                    if b == 0 and way_out:
                        y_clip(t - 2, 2)
                        y_clip(t - 2, 3)
                    if b == 1 and last:
                        x1_make(1)
                    if b == 1 and first:
                        x_style(t + 1, 0)
                        x_style(t + 1, 1)
                    if b == 1 and last:
                        x1_make(2)
                    if b == 1 and first:
                        x_style(t + 1, 2)
                    if b == 3 and last:
                        y_clip(t - 1, 0)

            loop = whole_run(iteration)
            loop(dve)
            for t in range(G - 2, G + 2):
                iteration(t, t % 2)

        @block.tensor
        def _(pe):
            pe.wait_ge(const_step, 6)
            pe.wait_ge(small_loaded, 16 * 7)
            for s in range(SC):
                ins = nc.tensor.transpose(ps_norm[:, s, :], cond_nat[:, P * s:P * (s + 1)], ident[:])
            ins.then_inc(small_turned, 1)
            nc.tensor.transpose(ps_attn[:, 0, 0:6 * C], bias_rows, ident[0:6 * C, 0:6 * C])\
              .then_inc(small_turned, 1)
            for m in range(3):
                pe.wait_ge(aff_loaded[m], 16)
                for s in range(SC):
                    wait(pe, aff_kept, SC * (m - 1) + s + 1 if m else 0)
                    for c in range(C):
                        ins = nc.tensor.transpose(ps_gen[4 + s][:, P * c:P * (c + 1)],
                                                  aff_nat[m][:, c, P * s:P * (s + 1)], ident[:])
                    ins.then_inc(aff_turned, 1)
                pe.wait_ge(aff_kept, SC * (m + 1))
                pe.wait_ge(small_kept, 3)
                wait(pe, style_made, m)
                for c in range(C):
                    for s in range(SC):
                        ins = nc.tensor.matmul(ps_attn[:, c, :], aff_t[:, s, P * c:P * (c + 1)], cond_t[:, s, :],
                                               start=(s == 0), stop=(s == SC - 1))
                ins.then_inc(style_summed, 1)
                pe.wait_ge(w_loaded[m], 16)
                for i in range(C):
                    wait(pe, w_low_made, C * (m - 1) + i + 1 if m else 0)
                    for o in range(C):
                        ins = nc.tensor.transpose(ps_gen[i][:, P * o:P * (o + 1)],
                                                  w_nat[m][:, o, P * i:P * (i + 1)], ident[:])
                    ins.then_inc(w_turned, 1)
                pe.wait_ge(w_squared, C * (m + 1))
                pe.wait_ge(style_squared, m + 1)
                wait(pe, norm_kept, m)
                for o in range(C):
                    for i in range(C):
                        ins = nc.tensor.matmul(ps_norm[:, o, :], w_sq[m][:, i, P * o:P * (o + 1)],
                                               style_sq[:, i, :], start=(i == 0), stop=(i == C - 1))
                ins.then_inc(norm_summed, 1)
            pe.wait_ge(w_low_made, 3 * C)
            pe.wait_ge(mods_ready, 3)

            drained = [None] * len(ps_gen)

            def take(bank, reader, count):
                if drained[bank]:
                    pe.wait_ge(*drained[bank])
                drained[bank] = (reader, count)
                return ps_gen[bank]

            def x_turn(t, c):
                if c == 0:
                    pe.wait_ge(x_loaded, 16 * t + 16)
                ps = take(BANK_X[c], x_res_made, C * t + c + 1)
                for b in range(GB):
                    ins = nc.tensor.transpose(ps[:, N * b:N * (b + 1)], x_in[:, b, P * c:P * (c + 1)], ident[:])
                ins.then_inc(x_turned, 1)

            def project(ps, m, c, high, low, part_ready=None):
                for i in range(C):
                    if part_ready:
                        pe.wait_ge(part_ready[0], part_ready[1] + i + 1)
                    for k, (w, a) in enumerate(((w_high[m], high), (w_low[m], high), (w_high[m], low))):
                        ins = nc.tensor.matmul(ps[:], w[:, i, P * c:P * (c + 1)], a(i),
                                               start=(i == 0 and k == 0), stop=(i == C - 1 and k == 2))
                return ins

            def k_project(t, c):
                project(take(BANK_K[c], keys_made, C * t + c + 1), K_MAT, c, lambda i: xm_high[:, i, :],
                        lambda i: xm_low[:, i, :], (xm_low_made, C * t) if c == 0 else None)\
                    .then_inc(keys_summed, 1)

            def keys_turn(t, b):
                pe.wait_ge(keys_made, C * t + C)
                ps = take(BANK_KN[b], keys_strip_made, GB * t + b + 1)
                for c in range(C):
                    ins = nc.tensor.transpose(ps[:, P * c:P * (c + 1)], keys[:, c, b, :], ident[:])
                ins.then_inc(keys_turned, 1)

            def block_items(b, k, count):
                return keys_strip[:, b, PAIR * k:PAIR * (k + count), :].rearrange("p n h -> p (n h)")

            def scores(t, b):
                n = GB * t + b
                pe.wait_ge(keys_spread_made, 64 * n + 64)
                wait(pe, shifted, n)
                nc.tensor.matmul(ps_scores[:], flat(same_lhs), flat(same_rhs),
                                 start=True, stop=False, skip_group_check=True)
                for q in range(Q):
                    for c in range(QUADS):
                        k = QUADS * q + c
                        ins = nc.tensor.matmul(ps_scores[HD * c:HD * (c + 1), STRIPS * q:STRIPS * (q + 1), :],
                                               block_items(b, k, 1), keys_spread[:, :, HD * k:HD * (k + 1)],
                                               start=False, stop=True, skip_group_check=True)
                ins.then_inc(scores_ready, 1)

            def items_turn(t, b):
                ps = take(BANK_ITEMS[b], keys_item_made, GB * t + b + 1)
                for q in range(Q):
                    ins = nc.tensor.transpose(ps[:, P * q:P * (q + 1)], block_items(b, QUADS * q, QUADS), ident[:])
                ins.then_inc(items_turned, 1)

            def attend(t, b):
                n = GB * t + b
                pe.wait_ge(keys_item_made, n + 1)
                pe.wait_ge(probs_spread_made, 64 * n + 64)
                wait(pe, attn_nat_made, n)
                for q in range(Q):
                    for s in range(STRIPS):
                        k = STRIPS * q + s
                        ins = nc.tensor.matmul(ps_attn[HD * s:HD * (s + 1), q, :],
                                               keys_item[:, q, HD * s:HD * (s + 1)],
                                               probs_spread[:, :, HD * k:HD * (k + 1)], start=True, stop=True)
                ins.then_inc(attn_summed, 1)

            def attn_turn(t, b):
                pe.wait_ge(attn_nat_made, GB * t + b + 1)
                ps = take(BANK_ATTN[b], attn_styled, GB * t + b + 1)
                for c in range(C):
                    ins = nc.tensor.transpose(ps[:, P * c:P * (c + 1)], flat(attn_nat)[:, P * c:P * (c + 1)],
                                              ident[:])
                ins.then_inc(attn_turned, 1)

            def o_project(t, c):
                if c == 0:
                    pe.wait_ge(attn_low_made, GB * t + GB)
                project(take(BANK_O[c], x1_made, C * t + c + 1), O_MAT, c,
                        lambda i: attn_high[:, i].rearrange("p b n -> p (b n)"),
                        lambda i: attn_low[:, i].rearrange("p b n -> p (b n)")).then_inc(o_summed, 1)

            def l_project(t, c):
                project(take(BANK_L[c], y_made, C * t + c + 1), L_MAT, c, lambda i: x1m_high[:, i, :],
                        lambda i: x1m_low[:, i, :], (x1m_low_made, C * t) if c == 0 else None)\
                    .then_inc(l_summed, 1)

            def x2_turn(t, b):
                if b == 0:
                    pe.wait_ge(x2_made, C * t + C)
                ps = take(BANK_OUT[b], x_out_made, GB * t + b + 1)
                for c in range(C):
                    ins = nc.tensor.transpose(ps[:, P * c:P * (c + 1)], x1[:, c, b, :], ident[:])
                ins.then_inc(x2_turned, 1)

            for c in range(C):
                x_turn(0, c)
            for c in range(C):
                k_project(0, c)
            keys_turn(0, 0)
            keys_turn(0, 1)

            def iteration(t, p):
                attends, first, last, way_out = parts(t)
                for b in range(GB):
                    n_t, n_b = (t - 1, GB - 1) if b == 0 else (t, b - 1)
                    before = last if b == 0 else attends
                    if attends:
                        scores(t, b)
                    if b == 0 and way_out:
                        l_project(t - 2, 2)
                    if b == 1 and last:
                        o_project(t - 1, 0)
                    if b == 2 and last:
                        o_project(t - 1, 3)
                    if b == 3 and first:
                        k_project(t + 1, 2)
                        k_project(t + 1, 3)
                    if before:
                        attend(n_t, n_b)
                    if attends:
                        items_turn(t, b)
                    if b == 0 and attends:
                        keys_turn(t, 2)
                        keys_turn(t, 3)
                    if b == 1 and way_out:
                        for i in range(GB):
                            x2_turn(t - 2, i)
                    if b == 1 and last:
                        o_project(t - 1, 1)
                    if b == 3 and first:
                        keys_turn(t + 1, 0)
                    if b == 3 and last:
                        l_project(t - 1, 0)
                    if b == 2 and first:
                        k_project(t + 1, 0)
                    if before:
                        attn_turn(n_t, n_b)
                    if b == 0 and way_out:
                        l_project(t - 2, 3)
                    if b == 1 and first:
                        x_turn(t + 1, 0)
                        x_turn(t + 1, 1)
                    if b == 1 and last:
                        o_project(t - 1, 2)
                    if b == 1 and first:
                        x_turn(t + 1, 2)
                        x_turn(t + 1, 3)
                    if b == 2 and first:
                        k_project(t + 1, 1)
                    if b == 3 and last:
                        l_project(t - 1, 1)
                    if b == 3 and first:
                        keys_turn(t + 1, 1)

            iteration(0, 0)
            iteration(1, 1)
            left = list(drained)

            def left_before(t):
                return [(reader, count + C * (t - 2)) for reader, count in left]

            with pe.Fori(1, G // 2 - 1) as pair:
                drained[:] = left_before(pair * 2)
                iteration(pair * 2, 0)
                iteration(pair * 2 + 1, 1)
            assert [reader for reader, _ in drained] == [reader for reader, _ in left]
            drained[:] = left_before(G - 2)
            for t in range(G - 2, G + 2):
                iteration(t, t % 2)


_INS = ["x", "cond_512", "L0_cond_k_aff_w", "L0_cond_k_aff_b", "L0_cond_k_w", "L0_cond_k_b",
        "L0_cond_o_aff_w", "L0_cond_o_aff_b", "L0_cond_o_w", "L0_cond_o_b",
        "L1_cond_weight", "L1_cond_bias", "L1_cond_affine_w", "L1_cond_affine_b"]


def kernel(**inputs):
    import numpy as _np
    import concourse.bacc as _bacc
    from concourse.bass_utils import run_bass_kernel_spmd as _run

    nc = _bacc.Bacc("TRN2", target_bir_lowering=False, num_devices=1)
    arrays, args = {}, []
    for name in _INS:
        a = _np.ascontiguousarray(inputs[name])
        arrays[f"in_{name}_dram"] = a
        args.append(nc.dram_tensor(f"in_{name}_dram", a.shape, mybir.dt.from_np(a.dtype), kind="ExternalInput").ap())
    shape = inputs["x"].shape
    args.append(nc.dram_tensor("out_dram", shape, F32, kind="ExternalOutput").ap())
    modulated_chain_kernel(nc, *args)
    r = _run(nc, [arrays], core_ids=[0])
    return r.results[0]["out_dram"]
```

```python
from contextlib import ExitStack

import concourse.bass as bass
from concourse import mybir

F32 = mybir.dt.float32
F32R = mybir.dt.float32r
ALU = mybir.AluOpType
ACT = mybir.ActivationFunctionType
AX_X = mybir.AxisListType.X

P = 128
HD = 32
EPS = 1e-8
CLAMP = 256.0
MASKED = -1e30

K_STYLE, O_STYLE, L_STYLE, K_DEMOD, O_DEMOD, L_DEMOD = range(6)
K_MAT, O_MAT, L_MAT = range(3)

BANK_K = (1, 2, 0, 1)
BANK_O = (2, 0, 1, 2)
BANK_L = (2, 0, 1, 0)
BANK_ITEMS = (3, 5, 3, 5)
BANK_ATTN = (4, 4, 4, 4)
BANK_OUT = (3, 4, 5, 3)
BANK_X = (5, 3, 4, 0)
BANK_AFF = (0, 1)
BANK_STYLE = 2
BANK_W = (0, 1, 2, 0)
BANK_NORM = 1
BANK_SPREAD = (3, 4, 5, 3)
BANK_BIAS = 4


def modulated_chain_kernel(nc, x, cond, k_aff_w, k_aff_b, k_w, k_b, o_aff_w, o_aff_b, o_w, o_b,
                           l_w, l_b, l_aff_w, l_aff_b, out):
    B, N, F = x.shape
    S = cond.shape[1]
    C = F // P
    GB = 512 // N
    G = B // GB
    SC = S // P
    H = F // HD
    STRIPS = P // HD
    QUADS = P // HD
    PAIR = HD // H
    Q = HD // PAIR // QUADS
    SCALE = 1.0 / float(HD) ** 0.5
    GAIN = 1.0 / float(S) ** 0.5
    assert N == P and B == P and C == 4 and GB == 4 and Q == 4 and G % 2 == 0
    assert HD == 32 and PAIR * H == HD

    with ExitStack() as ctx:
        def sb(name, shape, dt=F32):
            return ctx.enter_context(nc.sbuf_tensor(name, shape, dt))

        def sem(name):
            return ctx.enter_context(nc.semaphore(name))

        w_high = [sb(f"w_high{m}", [P, C, F], F32R) for m in range(3)]
        w_low = [sb(f"w_low{m}", [P, C, F], F32R) for m in range(3)]
        mods = sb("mods", [P, 6, C, B])
        bias = sb("bias", [P, 6, C])
        ident = sb("ident", [P, P])
        mask = sb("mask", [P, Q * STRIPS, PAIR, H])

        x_in = sb("x_in", [P, GB, F])
        x_res = [sb(f"x_res{p}", [P, C, GB, N]) for p in range(2)]
        xm = sb("xm", [P, 2, GB * N])
        xm_high = sb("xm_high", [P, C, GB * N], F32R)
        xm_low = sb("xm_low", [P, C, GB * N], F32R)
        strip_demod = sb("strip_demod", [P, H, B])
        strip_bias = sb("strip_bias", [P, H])
        keys_strip = sb("keys_strip", [P, GB, HD, H])
        keys_spread = sb("keys_spread", [P, STRIPS, HD * H])
        keys_item = sb("keys_item", [P, Q, P])
        row_max = sb("row_max", [P, Q * STRIPS])
        row_sum = sb("row_sum", [P, Q * STRIPS])
        row_inv = sb("row_inv", [P, Q * STRIPS])
        soft = sb("soft", [P, Q * STRIPS, HD])
        probs = sb("probs", [P, Q * STRIPS, HD])
        probs_spread = sb("probs_spread", [P, QUADS, Q * STRIPS * HD])
        attn_nat = sb("attn_nat", [P, H, HD])
        attn = sb("attn", [P, C, N])
        attn_high = sb("attn_high", [P, C, GB, N], F32R)
        attn_low = sb("attn_low", [P, C, GB, N], F32R)
        x1 = sb("x1", [P, C, GB, N])
        x1m = sb("x1m", [P, 2, GB * N])
        x1m_high = sb("x1m_high", [P, C, GB * N], F32R)
        x1m_low = sb("x1m_low", [P, C, GB * N], F32R)
        y = sb("y", [P, 2, GB, N])
        x_out = sb("x_out", [P, GB, F])

        ps_scores = ctx.enter_context(nc.psum_tensor("ps_scores", [P, Q * STRIPS, HD], F32))
        ps_attn = ctx.enter_context(nc.psum_tensor("ps_attn", [P, Q, P], F32))
        ps_gen = [ctx.enter_context(nc.psum_tensor(f"ps_gen{i}", [P, 512], F32)) for i in range(6)]

        small_loaded = sem("small_loaded")
        aff_loaded = [sem(f"aff_loaded{m}") for m in range(3)]
        w_loaded = [sem(f"w_loaded{m}") for m in range(3)]
        const_step = sem("const_step")
        small_turned = sem("small_turned")
        small_kept = sem("small_kept")
        aff_turned = sem("aff_turned")
        aff_kept = sem("aff_kept")
        style_summed = sem("style_summed")
        style_made = sem("style_made")
        style_squared = sem("style_squared")
        w_turned = sem("w_turned")
        w_squared = sem("w_squared")
        w_low_made = sem("w_low_made")
        norm_summed = sem("norm_summed")
        norm_kept = sem("norm_kept")
        norm_step = sem("norm_step")
        root_made = sem("root_made")
        mods_ready = sem("mods_ready")
        copier_made = sem("copier_made")
        strip_summed = sem("strip_summed")
        strip_kept = sem("strip_kept")

        x_loaded = sem("x_loaded")
        x_turned = sem("x_turned")
        xm_made = sem("xm_made")
        x_res_made = sem("x_res_made")
        xm_high_made = sem("xm_high_made")
        xm_low_made = sem("xm_low_made")
        keys_summed = sem("keys_summed")
        keys_blocked = sem("keys_blocked")
        keys_scaled = sem("keys_scaled")
        keys_strip_made = sem("keys_strip_made")
        items_turned = sem("items_turned")
        keys_spread_made = sem("keys_spread_made")
        keys_item_made = sem("keys_item_made")
        scores_ready = sem("scores_ready")
        scores_masked = sem("scores_masked")
        max_made = sem("max_made")
        shifted = sem("shifted")
        exp_made = sem("exp_made")
        sum_made = sem("sum_made")
        sum_inverted = sem("sum_inverted")
        soft_made = sem("soft_made")
        probs_made = sem("probs_made")
        probs_spread_made = sem("probs_spread_made")
        attn_summed = sem("attn_summed")
        attn_nat_made = sem("attn_nat_made")
        attn_turned = sem("attn_turned")
        attn_styled = sem("attn_styled")
        attn_high_made = sem("attn_high_made")
        attn_low_made = sem("attn_low_made")
        o_summed = sem("o_summed")
        x1_made = sem("x1_made")
        x1m_made = sem("x1m_made")
        x1m_high_made = sem("x1m_high_made")
        x1m_low_made = sem("x1m_low_made")
        l_summed = sem("l_summed")
        y_made = sem("y_made")
        y_clipped = sem("y_clipped")
        x2_made = sem("x2_made")
        x2_turned = sem("x2_turned")
        x_out_made = sem("x_out_made")
        out_stored = sem("out_stored")
        spread_zeroed = sem("spread_zeroed")

        def over_n(ap, groups):
            return ap.unsqueeze(2).to_broadcast([P, groups, N])

        def batches(t):
            return bass.ds(GB * t, GB) if not isinstance(t, int) else slice(GB * t, GB * t + GB)

        def starts(t):
            return isinstance(t, int) and t == 0

        def column(n):
            return bass.ds(n, 1) if not isinstance(n, int) else slice(n, n + 1)

        def wait(eng, semaphore, value):
            if not isinstance(value, int) or value > 0:
                eng.wait_ge(semaphore, value)

        def whole_run(iteration):
            iteration(0, 0)
            iteration(1, 1)

            def loop(eng):
                with eng.Fori(1, G // 2 - 1) as pair:
                    iteration(pair * 2, 0)
                    iteration(pair * 2 + 1, 1)
            return loop

        def parts(t):
            if not isinstance(t, int):
                return True, True, True, True
            return t < G, t + 1 < G, 1 <= t <= G, 2 <= t <= G + 1

        def flat(tile):
            dims = " ".join("abc"[:len(tile.shape) - 1])
            return tile[:] if len(tile.shape) == 2 else tile[:].rearrange(f"p {dims} -> p ({dims})")

        aff_nat = [flat(a).rearrange("p (c s) -> p c s", c=C) for a in (xm, x1m, x1m)]
        w_nat = [flat(a).rearrange("p (c f) -> p c f", c=C) for a in (probs_spread, x1, x1)]
        w_sq = [flat(a).rearrange("p (c f) -> p c f", c=C) for a in (keys_strip, x_out, x_out)]
        aff_t = flat(x_res[1])[:, 0:SC * F].rearrange("p (s f) -> p s f", s=SC)
        cond_t = flat(x_res[1])[:, SC * F:SC * (F + B)].rearrange("p (s b) -> p s b", s=SC)
        cond_nat = flat(attn_nat)[:, 0:S]
        bias_rows = flat(attn_nat)[0:6 * C, S:S + P]
        copier = flat(attn).rearrange("p (g s d) -> p g s d", g=QUADS, s=STRIPS)
        style_sq = flat(y)[:, 0:C * B].rearrange("p (c b) -> p c b", c=C)
        root, newton = [[a.rearrange("p (c b) -> p c b", c=C) for a in pair] for pair in
                        ((flat(keys_item), flat(x1m)[:, 0:C * B], flat(x_out)[:, 0:C * B]),
                         (flat(soft), flat(x1m)[:, C * B:], flat(x_out)[:, C * B:2 * C * B]))]

        block = ctx.enter_context(nc.Block())

        @block.sync
        def _(sp):
            sp.dma_start(cond_nat, cond).then_inc(small_loaded, 16)
            for i, vec in enumerate((k_aff_b, o_aff_b, l_aff_b, k_b, o_b, l_b)):
                sp.dma_start(bias_rows[C * i:C * (i + 1), :], vec.rearrange("(c p) -> c p", p=P))\
                  .then_inc(small_loaded, 16)

            def load_matrix(m):
                aff, w = ((k_aff_w, k_w), (o_aff_w, o_w), (l_aff_w, l_w))[m]
                wait(sp, aff_turned, SC * m if m == L_MAT else 0)
                sp.dma_start(aff_nat[m], aff.rearrange("(c p) s -> p c s", p=P)).then_inc(aff_loaded[m], 16)
                wait(sp, w_turned, C * m if m == L_MAT else 0)
                sp.dma_start(w_nat[m], w.rearrange("(c p) f -> p c f", p=P)).then_inc(w_loaded[m], 16)

            load_matrix(K_MAT)

            def load_x(t):
                wait(sp, x_turned, C * t)
                sp.dma_start(x_in[:], x[batches(t)].rearrange("b n f -> n b f")).then_inc(x_loaded, 16)

            def store_out(t):
                sp.wait_ge(x_out_made, GB * t + GB)
                sp.dma_start(out[batches(t)].rearrange("b n f -> n b f"), x_out[:]).then_inc(out_stored, 16)

            def spread_keys(t, b):
                n = GB * t + b
                if b == 0:
                    sp.wait_ge(keys_strip_made, n + 1)
                wait(sp, scores_ready, n)
                for s in range(STRIPS):
                    strip = slice(HD * s, HD * s + HD)
                    sp.dma_start(keys_spread[strip, s, :], keys_strip[strip, b].rearrange("p n h -> p (n h)"))\
                      .then_inc(keys_spread_made, 16)
                if b < GB - 1:
                    sp.wait_ge(keys_strip_made, n + 2)

            def spread_probs(t, b):
                n = GB * t + b
                sp.wait_ge(probs_made, n + 1)
                wait(sp, attn_summed, n)
                for s in range(QUADS):
                    quad = slice(HD * s, HD * s + HD)
                    sp.dma_start(probs_spread[quad, s, :], probs[quad].rearrange("p k h -> p (k h)"))\
                      .then_inc(probs_spread_made, 16)

            load_x(0)
            load_matrix(O_MAT)
            sp.wait_ge(spread_zeroed, 1)
            spread_keys(0, 0)

            def iteration(t, p):
                attends, first, _, way_out = parts(t)
                if first and isinstance(t, int) and t == 0:
                    load_x(1)
                for b in range(GB):
                    if attends and b < GB - 1:
                        spread_keys(t, b + 1)
                    if first and b == GB - 1:
                        spread_keys(t + 1, 0)
                    if attends:
                        if isinstance(t, int) and t == 0 and b == 0:
                            sp.wait_ge(spread_zeroed, 2)
                        spread_probs(t, b)
                    if b == 0 and starts(t):
                        load_matrix(L_MAT)
                    if b == 1 and way_out:
                        store_out(t - 2)
                    if b == 2 and (not isinstance(t, int) or t + 2 < G):
                        load_x(t + 2)

            loop = whole_run(iteration)
            loop(sp)
            for t in range(G - 2, G + 2):
                iteration(t, t % 2)
            sp.wait_ge(out_stored, 16 * G)

        @block.gpsimd
        def _(pool):
            nc.gpsimd.memset(ident[:], 0.0).then_inc(const_step, 1)
            pool.wait_ge(const_step, 1)
            nc.gpsimd.affine_select(out=ident[:], in_=ident[:], compare_op=ALU.not_equal, fill=1.0, base=0,
                                    pattern=[[-1, P]], channel_multiplier=1).then_inc(const_step, 1)
            nc.gpsimd.memset(mask[:], 0.0).then_inc(const_step, 1)
            for quad in range(QUADS):
                rows = mask[HD * quad:HD * (quad + 1)]
                for side in (1, -1):
                    pool.wait_ge(const_step, 3 + 2 * quad + (side < 0))
                    nc.gpsimd.affine_select(out=rows, in_=rows, compare_op=ALU.is_ge, fill=MASKED,
                                            base=0 if side > 0 else H - 1,
                                            pattern=[[0, Q * STRIPS], [-side * H, PAIR], [0, H]],
                                            channel_multiplier=side).then_inc(const_step, 1)
            pool.wait_ge(const_step, 3 + 2 * QUADS)
            nc.gpsimd.memset(keys_spread[:], 0.0).then_inc(spread_zeroed, 1)

            def x_low(t, c):
                pool.wait_ge(xm_high_made, C * t + c + 1)
                wait(pool, keys_summed, C * t)
                nc.gpsimd.tensor_tensor(xm_low[:, c, :], xm[:, c % 2, :], xm_high[:, c, :],
                                        ALU.subtract).then_inc(xm_low_made, 1)

            def keys_bias(t, b):
                pool.wait_ge(keys_scaled, GB * t + b + 1)
                nc.gpsimd.tensor_tensor(keys_strip[:, b], keys_strip[:, b],
                                        strip_bias[:].unsqueeze(1).to_broadcast([P, HD, H]),
                                        ALU.add).then_inc(keys_strip_made, 1)

            def normalise(t, b):
                pool.wait_ge(sum_inverted, GB * t + b + 1)
                nc.gpsimd.tensor_tensor(soft[:], soft[:], row_inv[:].unsqueeze(2).to_broadcast(soft.shape),
                                        ALU.mult).then_inc(soft_made, 1)

            def attn_split(t, b):
                pool.wait_ge(attn_high_made, GB * t + b + 1)
                wait(pool, o_summed, C * t)
                nc.gpsimd.tensor_tensor(attn_low[:, :, b, :], attn[:], attn_high[:, :, b, :],
                                        ALU.subtract).then_inc(attn_low_made, 1)

            def x1_low(t, c):
                pool.wait_ge(x1m_high_made, C * t + c + 1)
                nc.gpsimd.tensor_tensor(x1m_low[:, c, :], x1m[:, c % 2, :], x1m_high[:, c, :],
                                        ALU.subtract).then_inc(x1m_low_made, 1)

            def x2_add(t, c):
                pool.wait_ge(y_clipped, C * t + c + 1)
                nc.gpsimd.tensor_tensor(x1[:, c], y[:, c % 2], x1[:, c], ALU.add).then_inc(x2_made, 1)

            for c in range(C):
                x_low(0, c)
            nc.gpsimd.memset(probs_spread[:], 0.0).then_inc(spread_zeroed, 1)
            pool.wait_ge(strip_kept, QUADS + 1)
            for b in range(GB):
                keys_bias(0, b)

            def iteration(t, p):
                attends, first, last, way_out = parts(t)
                for b in range(GB):
                    if b == 2 and first:
                        x_low(t + 1, 2)
                        x_low(t + 1, 3)
                    if b == 3 and first:
                        keys_bias(t + 1, 1)
                    if attends:
                        normalise(t, b)
                    if b == 3 and first:
                        keys_bias(t + 1, 2)
                        keys_bias(t + 1, 3)
                    if b == 0 and way_out:
                        x2_add(t - 2, 1)
                    if b == 0 and last:
                        attn_split(t - 1, 3)
                    if b == 0 and way_out:
                        x2_add(t - 2, 2)
                        x2_add(t - 2, 3)
                    if b == 1 and last:
                        x1_low(t - 1, 0)
                        x1_low(t - 1, 1)
                    if b == 1 and first:
                        x_low(t + 1, 0)
                        x_low(t + 1, 1)
                    if b == 2 and attends:
                        attn_split(t, 0)
                        attn_split(t, 1)
                    if b == 2 and last:
                        x1_low(t - 1, 2)
                        x1_low(t - 1, 3)
                    if b == 2 and first:
                        keys_bias(t + 1, 0)
                    if b == 3 and attends:
                        attn_split(t, 2)
                    if b == 3 and last:
                        x2_add(t - 1, 0)

            loop = whole_run(iteration)
            loop(pool)
            for t in range(G - 2, G + 2):
                iteration(t, t % 2)

        @block.scalar
        def _(act):
            def style_keep(m):
                act.wait_ge(small_kept, 3)
                act.wait_ge(style_summed, m + 1)
                for c in range(C):
                    ins = nc.scalar.activation(mods[:, K_STYLE + m, c, :], ps_gen[BANK_STYLE][:, B * c:B * (c + 1)],
                                               ACT.Identity, bias=bias[:, m, c:c + 1],
                                               scale=GAIN if m == L_MAT else 1.0)
                ins.then_inc(style_made, 1)

            def w_round(m):
                for i in range(C):
                    act.wait_ge(w_turned, C * m + i + 1)
                    nc.scalar.activation(w_high[m][:, i, :], ps_gen[BANK_W[i]][:], ACT.Copy)
                    nc.scalar.activation(w_sq[m][:, i, :], ps_gen[BANK_W[i]][:], ACT.Square).then_inc(w_squared, 1)

            def norm_root(m):
                act.wait_ge(norm_kept, m + 1)
                wait(act, mods_ready, m)
                nc.scalar.activation(root[m], mods[:, K_DEMOD + m], ACT.Sqrt).then_inc(root_made, 1)

            def x_keep(t, c, p):
                act.wait_ge(xm_made, C * t + c + 1)
                wait(act, keys_summed, C * t)
                nc.scalar.activation(xm_high[:, c, :], xm[:, c % 2, :], ACT.Copy).then_inc(xm_high_made, 1)
                wait(act, x1_made, C * (t - 2) + c + 1 if not isinstance(t, int) or t >= 2 else 0)
                ins = nc.scalar.activation(x_res[p][:, c].rearrange("p b n -> p (b n)"), ps_gen[BANK_X[c]][:],
                                           ACT.Identity, bias=bias[:, 3 + O_MAT, c:c + 1])
                ins.then_inc(x_res_made, 1)

            def strips_keep():
                heads = strip_demod[:].rearrange("p (c g) b -> p c g b", g=QUADS)
                for g in range(QUADS):
                    act.wait_ge(strip_summed, g + 1)
                    nc.scalar.activation(heads[:, :, g, :], ps_gen[BANK_SPREAD[g]][:].rearrange(
                        "p (c b) -> p c b", c=C), ACT.Copy).then_inc(strip_kept, 1)
                act.wait_ge(strip_summed, QUADS + 1)
                nc.scalar.activation(strip_bias[:].rearrange("p (c g) -> p g c", g=QUADS),
                                     ps_gen[BANK_BIAS][:, 0:H].rearrange("p (g c) -> p g c", g=QUADS), ACT.Copy)\
                  .then_inc(strip_kept, 1)

            def items_keep(t, b):
                act.wait_ge(items_turned, GB * t + b + 1)
                wait(act, attn_summed, GB * t + b)
                nc.scalar.activation(flat(keys_item), ps_gen[BANK_ITEMS[b]][:], ACT.Copy)\
                  .then_inc(keys_item_made, 1)

            def exp(t, b):
                act.wait_ge(shifted, GB * t + b + 1)
                nc.scalar.activation(soft[:], soft[:], ACT.Exp, scale=SCALE).then_inc(exp_made, 1)

            def attn_round(t, b):
                act.wait_ge(attn_styled, GB * t + b + 1)
                wait(act, o_summed, C * t)
                nc.scalar.activation(attn_high[:, :, b, :], attn[:], ACT.Copy).then_inc(attn_high_made, 1)

            def x1_round(t, c):
                act.wait_ge(x1m_made, C * t + c + 1)
                wait(act, l_summed, C * t)
                nc.scalar.activation(x1m_high[:, c, :], x1m[:, c % 2, :], ACT.Copy).then_inc(x1m_high_made, 1)

            def y_scale(t, c):
                act.wait_ge(l_summed, C * t + c + 1)
                wait(act, x2_made, C * t + c - 1)
                for b in range(GB):
                    ins = nc.scalar.activation(y[:, c % 2, b, :], ps_gen[BANK_L[c]][:, N * b:N * (b + 1)],
                                               ACT.Identity, bias=bias[:, 3 + L_MAT, c:c + 1],
                                               scale=mods[:, L_DEMOD, c, column(GB * t + b)])
                ins.then_inc(y_made, 1)

            def out_keep(t, b):
                act.wait_ge(x2_turned, GB * t + b + 1)
                if b == 0:
                    wait(act, out_stored, 16 * t)
                nc.scalar.activation(x_out[:, b, :], ps_gen[BANK_OUT[b]][:], ACT.Copy).then_inc(x_out_made, 1)

            style_keep(K_MAT)
            w_round(K_MAT)
            for c in range(C):
                x_keep(0, c, 0)
            norm_root(K_MAT)
            strips_keep()

            def iteration(t, p):
                attends, first, last, way_out = parts(t)
                for b in range(GB):
                    if attends:
                        exp(t, b)
                    if b == 0 and way_out:
                        y_scale(t - 2, 2)
                    if b == 2 and first:
                        x_keep(t + 1, 3, 1 - p)
                    if b == 2 and attends:
                        attn_round(t, 0)
                    if attends:
                        items_keep(t, b)
                    if b == 0 and last:
                        attn_round(t - 1, 3)
                    if b == 0 and way_out:
                        y_scale(t - 2, 3)
                    if b == 0 and starts(t):
                        style_keep(O_MAT)
                        w_round(O_MAT)
                    if b == 1 and starts(t):
                        style_keep(L_MAT)
                        w_round(L_MAT)
                    if b == 1 and way_out:
                        for i in range(GB):
                            out_keep(t - 2, i)
                    if b == 1 and last:
                        x1_round(t - 1, 0)
                        x1_round(t - 1, 1)
                    if b == 1 and first:
                        x_keep(t + 1, 0, 1 - p)
                        x_keep(t + 1, 1, 1 - p)
                    if b == 1 and last:
                        x1_round(t - 1, 2)
                    if b == 1 and first:
                        x_keep(t + 1, 2, 1 - p)
                    if b == 2 and last:
                        x1_round(t - 1, 3)
                    if b == 2 and attends:
                        attn_round(t, 1)
                    if b == 3 and starts(t):
                        norm_root(O_MAT)
                    if b == 2 and starts(t - 1):
                        norm_root(L_MAT)
                    if b == 3 and starts(t - 1):
                        act.wait_ge(mods_ready, L_MAT + 1)
                    if b == 3 and last:
                        y_scale(t - 1, 0)
                    if b == 3 and attends:
                        attn_round(t, 2)
                    if b == 3 and last:
                        y_scale(t - 1, 1)

            loop = whole_run(iteration)
            loop(act)
            for t in range(G - 2, G + 2):
                iteration(t, t % 2)

        @block.vector
        def _(dve):
            dve.wait_ge(small_turned, 1)
            nc.vector.tensor_copy(cond_t, ps_gen[4][:, 0:SC * B].rearrange("p (s b) -> p s b", s=SC))\
              .then_inc(small_kept, 1)
            dve.wait_ge(small_turned, 2)
            nc.vector.tensor_copy(flat(bias), ps_attn[:, 0, 0:6 * C])\
              .then_inc(small_kept, 2)

            def aff_keep(m):
                for s in range(SC):
                    dve.wait_ge(aff_turned, SC * m + s + 1)
                    wait(dve, style_summed, m)
                    nc.vector.tensor_copy(aff_t[:, s, :], ps_gen[BANK_AFF[s]][:]).then_inc(aff_kept, 1)

            def style_square(m):
                dve.wait_ge(style_made, m + 1)
                wait(dve, norm_summed, m)
                nc.vector.tensor_tensor(style_sq, mods[:, K_STYLE + m], mods[:, K_STYLE + m], ALU.mult)\
                  .then_inc(style_squared, 1)

            def w_split(m):
                for i in range(C):
                    dve.wait_ge(w_squared, C * m + i + 1)
                    nc.vector.tensor_tensor(w_low[m][:, i, :], ps_gen[BANK_W[i]][:], w_high[m][:, i, :],
                                            ALU.subtract).then_inc(w_low_made, 1)

            def norm_keep(m):
                dve.wait_ge(norm_summed, m + 1)
                nc.vector.tensor_scalar(mods[:, K_DEMOD + m],
                                        ps_gen[BANK_NORM][:].rearrange("p (c b) -> p c b", c=C), EPS, None,
                                        ALU.add).then_inc(norm_kept, 1)

            def demodulate(m):
                norm = mods[:, K_DEMOD + m]
                dve.wait_ge(root_made, m + 1)
                nc.vector.reciprocal(root[m], root[m]).then_inc(norm_step, 1)
                dve.wait_ge(norm_step, 4 * m + 1)
                nc.vector.tensor_tensor(newton[m], root[m], root[m], ALU.mult).then_inc(norm_step, 1)
                dve.wait_ge(norm_step, 4 * m + 2)
                nc.vector.tensor_tensor(newton[m], newton[m], norm, ALU.mult).then_inc(norm_step, 1)
                dve.wait_ge(norm_step, 4 * m + 3)
                nc.vector.tensor_scalar(newton[m], newton[m], -0.5, 1.5, ALU.mult, ALU.add).then_inc(norm_step, 1)
                dve.wait_ge(norm_step, 4 * m + 4)
                nc.vector.tensor_tensor(norm, newton[m], root[m], ALU.mult).then_inc(mods_ready, 1)

            def x_style(t, c):
                dve.wait_ge(x_turned, C * t + c + 1)
                wait(dve, xm_low_made, C * t + c - 1)
                nc.vector.tensor_tensor(xm[:, c % 2, :].rearrange("p (b n) -> p b n", b=GB),
                                        ps_gen[BANK_X[c]][:].rearrange("p (b n) -> p b n", b=GB),
                                        over_n(mods[:, K_STYLE, c, batches(t)], GB),
                                        ALU.mult).then_inc(xm_made, 1)

            def shift(t, b):
                n = GB * t + b
                dve.wait_ge(scores_ready, n + 1)
                wait(dve, probs_made, n)
                nc.vector.tensor_tensor(soft[:], ps_scores[:], mask[:].rearrange("p k n h -> p k (n h)"),
                                        ALU.add).then_inc(scores_masked, 1)
                dve.wait_ge(scores_masked, n + 1)
                nc.vector.tensor_reduce(row_max[:], soft[:], AX_X, ALU.max).then_inc(max_made, 1)
                dve.wait_ge(max_made, n + 1)
                nc.vector.tensor_tensor(soft[:], soft[:], row_max[:].unsqueeze(2).to_broadcast(soft.shape),
                                        ALU.subtract).then_inc(shifted, 1)

            def row_sums(t, b):
                n = GB * t + b
                dve.wait_ge(exp_made, n + 1)
                nc.vector.tensor_reduce(row_sum[:], soft[:], AX_X, ALU.add).then_inc(sum_made, 1)
                dve.wait_ge(sum_made, n + 1)
                nc.vector.reciprocal(row_inv[:], row_sum[:]).then_inc(sum_inverted, 1)

            def probs_block(t, b):
                dve.wait_ge(soft_made, GB * t + b + 1)
                wait(dve, probs_spread_made, 64 * (GB * t + b))
                nc.vector.transpose(flat(probs), flat(soft)).then_inc(probs_made, 1)

            def keys_block(t, b):
                n = GB * t + b
                dve.wait_ge(keys_summed, n + 1)
                wait(dve, items_turned, GB * (t - 1) + b + 1 if not isinstance(t, int) or t > 0 else 0)
                nc.vector.transpose(keys_strip[:, b].rearrange("p n h -> p h n"),
                                    ps_gen[BANK_K[b]][:].rearrange("p (h d) -> p h d", h=H))\
                  .then_inc(keys_blocked, 1)

            def keys_scale(t, b):
                n = GB * t + b
                dve.wait_ge(keys_blocked, n + 1)
                if isinstance(t, int) and t == 0:
                    dve.wait_ge(strip_kept, QUADS)
                nc.vector.tensor_tensor(
                    keys_strip[:, b], keys_strip[:, b],
                    strip_demod[:, :, column(n)].rearrange("p h o -> p o h").to_broadcast([P, HD, H]),
                    ALU.mult).then_inc(keys_scaled, 1)

            def keys_make(t, b):
                keys_block(t, b)
                keys_scale(t, b)

            def attn_block(t, b):
                n = GB * t + b
                dve.wait_ge(attn_summed, n + 1)
                wait(dve, attn_turned, n)
                nc.vector.transpose(attn_nat[:], ps_attn[:].rearrange("p q (n h) -> p h (q n)", h=H))\
                  .then_inc(attn_nat_made, 1)

            def attn_style(t, b):
                dve.wait_ge(attn_turned, GB * t + b + 1)
                wait(dve, attn_low_made, GB * t + b)
                nc.vector.tensor_tensor(
                    attn[:], ps_gen[BANK_ATTN[b]][:].rearrange("p (c n) -> p c n", c=C),
                    mods[:, O_STYLE, :, column(GB * t + b)].to_broadcast([P, C, N]),
                    ALU.mult).then_inc(attn_styled, 1)

            def x1_add(t, c, p):
                dve.wait_ge(o_summed, C * t + c + 1)
                dve.wait_ge(x_res_made, C * t + c + 1)
                wait(dve, x2_turned, GB * t)
                for b in range(GB):
                    ins = nc.vector.scalar_tensor_tensor(
                        out=x1[:, c, b, :], in0=ps_gen[BANK_O[c]][:, N * b:N * (b + 1)],
                        scalar=mods[:, O_DEMOD, c, column(GB * t + b)], in1=x_res[p][:, c, b, :],
                        op0=ALU.mult, op1=ALU.add)
                ins.then_inc(x1_made, 1)

            def x1_style(t, c):
                dve.wait_ge(x1_made, C * t + c + 1)
                wait(dve, x1m_low_made, C * t + c - 1)
                nc.vector.tensor_tensor(x1m[:, c % 2, :].rearrange("p (b n) -> p b n", b=GB), x1[:, c],
                                        over_n(mods[:, L_STYLE, c, batches(t)], GB),
                                        ALU.mult).then_inc(x1m_made, 1)

            def y_clip(t, c):
                dve.wait_ge(y_made, C * t + c + 1)
                nc.vector.tensor_scalar(y[:, c % 2], y[:, c % 2], CLAMP, -CLAMP, ALU.min, ALU.max)\
                  .then_inc(y_clipped, 1)

            dve.wait_ge(const_step, 2)
            nc.vector.tensor_copy(copier, ident[:].rearrange("p (g d) -> p g d", g=QUADS).unsqueeze(2)
                                  .to_broadcast([P, QUADS, STRIPS, HD])).then_inc(copier_made, 1)
            aff_keep(K_MAT)
            style_square(K_MAT)
            w_split(K_MAT)
            for c in range(C):
                x_style(0, c)
            norm_keep(K_MAT)
            keys_block(0, 0)
            demodulate(K_MAT)
            keys_scale(0, 0)
            for b in range(1, GB):
                keys_make(0, b)
            dve.wait_ge(const_step, 3 + 2 * QUADS)

            def iteration(t, p):
                attends, first, last, way_out = parts(t)

                def x1_make(c):
                    x1_add(t - 1, c, 1 - p)
                    x1_style(t - 1, c)

                for b in range(GB):
                    n_t, n_b = (t - 1, GB - 1) if b == 0 else (t, b - 1)
                    before = last if b == 0 else attends
                    if attends:
                        shift(t, b)
                    if b == 3 and first:
                        keys_make(t + 1, 1)
                    if b == 2 and first:
                        x_style(t + 1, 3)
                    if b == 0 and starts(t):
                        aff_keep(O_MAT)
                    if b == 1 and starts(t):
                        norm_keep(O_MAT)
                        aff_keep(L_MAT)
                    if b == 2 and starts(t):
                        norm_keep(L_MAT)
                    if attends:
                        row_sums(t, b)
                    if b == 2 and last:
                        x1_add(t - 1, 3, 1 - p)
                    if b == 0 and way_out:
                        y_clip(t - 2, 1)
                    if attends and b == 3:
                        probs_block(t, b)
                    if b == 3 and first:
                        keys_make(t + 1, 2)
                    if before:
                        attn_block(n_t, n_b)
                    if attends and b < 3:
                        probs_block(t, b)
                    if b < 2 and starts(t):
                        style_square(O_MAT + b)
                        w_split(O_MAT + b)
                    if b == 1 and last:
                        x1_make(0)
                    if b == 2 and last:
                        x1_style(t - 1, 3)
                    if b == 3 and first:
                        keys_make(t + 1, 3)
                    if before:
                        attn_style(n_t, n_b)
                    if b == 2 and first:
                        keys_make(t + 1, 0)
                    if b == 0 and way_out:
                        y_clip(t - 2, 2)
                        y_clip(t - 2, 3)
                    if b == 1 and last:
                        x1_make(1)
                    if b == 1 and first:
                        x_style(t + 1, 0)
                        x_style(t + 1, 1)
                    if b == 1 and last:
                        x1_make(2)
                    if b == 1 and first:
                        x_style(t + 1, 2)
                    if b == 0 and starts(t - 1):
                        demodulate(O_MAT)
                        dve.wait_ge(mods_ready, O_MAT + 1)
                    if b == 3 and starts(t - 1):
                        demodulate(L_MAT)
                    if b == 3 and last:
                        y_clip(t - 1, 0)

            loop = whole_run(iteration)
            loop(dve)
            for t in range(G - 2, G + 2):
                iteration(t, t % 2)

        @block.tensor
        def _(pe):
            pe.wait_ge(const_step, 2)
            pe.wait_ge(small_loaded, 16 * 7)
            for s in range(SC):
                ins = nc.tensor.transpose(ps_gen[4][:, B * s:B * (s + 1)], cond_nat[:, P * s:P * (s + 1)], ident[:])
            ins.then_inc(small_turned, 1)
            nc.tensor.transpose(ps_attn[:, 0, 0:6 * C], bias_rows, ident[0:6 * C, 0:6 * C])\
              .then_inc(small_turned, 1)

            drained = [None] * len(ps_gen)

            def take(bank, reader, count):
                if drained[bank]:
                    pe.wait_ge(*drained[bank])
                drained[bank] = (reader, count)
                return ps_gen[bank]

            def aff_turn(m):
                pe.wait_ge(aff_loaded[m], 16)
                for s in range(SC):
                    ps = take(BANK_AFF[s], aff_kept, SC * m + s + 1)
                    for c in range(C):
                        ins = nc.tensor.transpose(ps[:, P * c:P * (c + 1)],
                                                  aff_nat[m][:, c, P * s:P * (s + 1)], ident[:])
                    ins.then_inc(aff_turned, 1)

            def style_sum(m):
                pe.wait_ge(aff_kept, SC * (m + 1))
                pe.wait_ge(small_kept, 3)
                ps = take(BANK_STYLE, style_made, m + 1)
                for c in range(C):
                    for s in range(SC):
                        ins = nc.tensor.matmul(ps[:, B * c:B * (c + 1)], aff_t[:, s, P * c:P * (c + 1)],
                                               cond_t[:, s, :], start=(s == 0), stop=(s == SC - 1))
                ins.then_inc(style_summed, 1)

            def w_turn(m):
                pe.wait_ge(w_loaded[m], 16)
                for i in range(C):
                    ps = take(BANK_W[i], w_low_made, C * m + i + 1)
                    for o in range(C):
                        ins = nc.tensor.transpose(ps[:, P * o:P * (o + 1)], w_nat[m][:, o, P * i:P * (i + 1)],
                                                  ident[:])
                    ins.then_inc(w_turned, 1)

            def norm_sum(m):
                pe.wait_ge(w_squared, C * (m + 1))
                pe.wait_ge(style_squared, m + 1)
                ps = take(BANK_NORM, norm_kept, m + 1)
                for o in range(C):
                    for i in range(C):
                        ins = nc.tensor.matmul(ps[:, B * o:B * (o + 1)], w_sq[m][:, i, P * o:P * (o + 1)],
                                               style_sq[:, i, :], start=(i == 0), stop=(i == C - 1))
                ins.then_inc(norm_summed, 1)

            def x_turn(t, c):
                if c == 0:
                    pe.wait_ge(x_loaded, 16 * t + 16)
                ps = take(BANK_X[c], x_res_made, C * t + c + 1)
                for b in range(GB):
                    ins = nc.tensor.transpose(ps[:, N * b:N * (b + 1)], x_in[:, b, P * c:P * (c + 1)], ident[:])
                ins.then_inc(x_turned, 1)

            def project(ps, m, c, high, low, part_ready=None, inputs=range(C)):
                for i in inputs:
                    if part_ready:
                        pe.wait_ge(part_ready[0], part_ready[1] + i + 1)
                    for k, (w, a) in enumerate(((w_high[m], high), (w_low[m], high), (w_high[m], low))):
                        ins = nc.tensor.matmul(ps[:], w[:, i, P * c:P * (c + 1)], a(i),
                                               start=(i == 0 and k == 0), stop=(i == C - 1 and k == 2))
                return ins

            def k_project(t, b):
                ps = take(BANK_K[b], keys_blocked, GB * t + b + 1)
                tokens = slice(N * b, N * (b + 1))
                for i in range(C):
                    if b == 0:
                        pe.wait_ge(xm_low_made, C * t + i + 1)
                    for k, (a, w) in enumerate(((xm_high, w_high), (xm_high, w_low), (xm_low, w_high))):
                        ins = nc.tensor.matmul(ps[:], a[:, i, tokens], w[K_MAT][:, i, :],
                                               start=(i == 0 and k == 0), stop=(i == C - 1 and k == 2))
                ins.then_inc(keys_summed, 1)

            def strips_sum():
                pe.wait_ge(mods_ready, K_MAT + 1)
                pe.wait_ge(copier_made, 1)
                for g in range(QUADS):
                    ps = take(BANK_SPREAD[g], strip_kept, g + 1)
                    nc.tensor.matmul(ps[:], copier[:, g].rearrange("p s d -> p (s d)"),
                                     mods[:, K_DEMOD].rearrange("p c b -> p (c b)"), start=True, stop=True)\
                      .then_inc(strip_summed, 1)
                ps = take(BANK_BIAS, strip_kept, QUADS + 1)
                for g in range(QUADS):
                    ins = nc.tensor.matmul(ps[:, C * g:C * (g + 1)], copier[:, g].rearrange("p s d -> p (s d)"),
                                           bias[:, 3 + K_MAT, :], start=True, stop=True)
                ins.then_inc(strip_summed, 1)

            def block_items(b, k, count):
                return keys_strip[:, b, PAIR * k:PAIR * (k + count), :].rearrange("p n h -> p (n h)")

            def scores(t, b):
                n = GB * t + b
                pe.wait_ge(keys_spread_made, 64 * n + 64)
                wait(pe, scores_masked, n)
                for q in range(Q):
                    for c in range(QUADS):
                        k = QUADS * q + c
                        ins = nc.tensor.matmul(ps_scores[HD * c:HD * (c + 1), STRIPS * q:STRIPS * (q + 1), :],
                                               block_items(b, k, 1), keys_spread[:, :, HD * k:HD * (k + 1)],
                                               start=True, stop=True)
                ins.then_inc(scores_ready, 1)

            def items_turn(t, b):
                ps = take(BANK_ITEMS[b], keys_item_made, GB * t + b + 1)
                for q in range(Q):
                    ins = nc.tensor.transpose(ps[:, P * q:P * (q + 1)], block_items(b, QUADS * q, QUADS), ident[:])
                ins.then_inc(items_turned, 1)

            def attend(t, b):
                n = GB * t + b
                pe.wait_ge(keys_item_made, n + 1)
                pe.wait_ge(probs_spread_made, 64 * n + 64)
                wait(pe, attn_nat_made, n)
                for q in range(Q):
                    for s in range(STRIPS):
                        k = STRIPS * q + s
                        ins = nc.tensor.matmul(ps_attn[HD * s:HD * (s + 1), q, :],
                                               keys_item[:, q, HD * s:HD * (s + 1)],
                                               probs_spread[:, :, HD * k:HD * (k + 1)], start=True, stop=True)
                ins.then_inc(attn_summed, 1)

            def attn_turn(t, b):
                pe.wait_ge(attn_nat_made, GB * t + b + 1)
                ps = take(BANK_ATTN[b], attn_styled, GB * t + b + 1)
                for c in range(C):
                    ins = nc.tensor.transpose(ps[:, P * c:P * (c + 1)], flat(attn_nat)[:, P * c:P * (c + 1)],
                                              ident[:])
                ins.then_inc(attn_turned, 1)

            def o_project(t, c):
                if c == 0:
                    pe.wait_ge(attn_low_made, GB * t + GB)
                project(take(BANK_O[c], x1_made, C * t + c + 1), O_MAT, c,
                        lambda i: attn_high[:, i].rearrange("p b n -> p (b n)"),
                        lambda i: attn_low[:, i].rearrange("p b n -> p (b n)")).then_inc(o_summed, 1)

            def l_project(t, c, inputs=range(C)):
                ps = take(BANK_L[c], y_made, C * t + c + 1) if inputs[0] == 0 else ps_gen[BANK_L[c]]
                ins = project(ps, L_MAT, c, lambda i: x1m_high[:, i, :], lambda i: x1m_low[:, i, :],
                              (x1m_low_made, C * t) if c == 0 else None, inputs)
                if inputs[-1] == C - 1:
                    ins.then_inc(l_summed, 1)

            def x2_turn(t, b):
                if b == 0:
                    pe.wait_ge(x2_made, C * t + C)
                ps = take(BANK_OUT[b], x_out_made, GB * t + b + 1)
                for c in range(C):
                    ins = nc.tensor.transpose(ps[:, P * c:P * (c + 1)], x1[:, c, b, :], ident[:])
                ins.then_inc(x2_turned, 1)

            aff_turn(K_MAT)
            style_sum(K_MAT)
            w_turn(K_MAT)
            for c in range(C):
                x_turn(0, c)
            norm_sum(K_MAT)
            pe.wait_ge(w_low_made, C)
            for b in range(GB - 1):
                k_project(0, b)
            strips_sum()
            k_project(0, GB - 1)

            def iteration(t, p):
                attends, first, last, way_out = parts(t)
                for b in range(GB):
                    n_t, n_b = (t - 1, GB - 1) if b == 0 else (t, b - 1)
                    before = last if b == 0 else attends
                    if attends:
                        scores(t, b)
                    if b == 0 and starts(t):
                        aff_turn(O_MAT)
                    if b == 1 and starts(t):
                        norm_sum(O_MAT)
                        aff_turn(L_MAT)
                    if b == 2 and starts(t):
                        norm_sum(L_MAT)
                    if b == 0 and way_out:
                        l_project(t - 2, 2)
                    if b == 1 and last:
                        o_project(t - 1, 0)
                    if b == 2 and last:
                        o_project(t - 1, 3)
                    if b == 3 and first:
                        k_project(t + 1, 2)
                        k_project(t + 1, 3)
                    if b == 3 and last and not first:
                        l_project(t - 1, 0)
                    if before:
                        attend(n_t, n_b)
                    if attends:
                        items_turn(t, b)
                    if b < 2 and starts(t):
                        style_sum(O_MAT + b)
                        w_turn(O_MAT + b)
                    if b == 1 and way_out:
                        for i in range(GB):
                            x2_turn(t - 2, i)
                    if b == 1 and last:
                        o_project(t - 1, 1)
                    if b == 3 and last and first:
                        l_project(t - 1, 0)
                    if b == 2 and first:
                        k_project(t + 1, 0)
                    if b == 0 and way_out:
                        l_project(t - 2, 3, range(1))
                    if before:
                        attn_turn(n_t, n_b)
                    if b == 0 and way_out:
                        l_project(t - 2, 3, range(1, C))
                    if b == 1 and first:
                        x_turn(t + 1, 0)
                        x_turn(t + 1, 1)
                    if b == 1 and last:
                        o_project(t - 1, 2)
                    if b == 1 and first:
                        x_turn(t + 1, 2)
                        x_turn(t + 1, 3)
                    if b == 2 and first:
                        k_project(t + 1, 1)
                    if b == 3 and last:
                        l_project(t - 1, 1)

            iteration(0, 0)
            iteration(1, 1)
            left = list(drained)

            def left_before(t):
                return [(reader, count + C * (t - 2)) for reader, count in left]

            with pe.Fori(1, G // 2 - 1) as pair:
                drained[:] = left_before(pair * 2)
                iteration(pair * 2, 0)
                iteration(pair * 2 + 1, 1)
            assert [reader for reader, _ in drained] == [reader for reader, _ in left]
            drained[:] = left_before(G - 2)
            for t in range(G - 2, G + 2):
                iteration(t, t % 2)


_INS = ["x", "cond_512", "L0_cond_k_aff_w", "L0_cond_k_aff_b", "L0_cond_k_w", "L0_cond_k_b",
        "L0_cond_o_aff_w", "L0_cond_o_aff_b", "L0_cond_o_w", "L0_cond_o_b",
        "L1_cond_weight", "L1_cond_bias", "L1_cond_affine_w", "L1_cond_affine_b"]


def kernel(**inputs):
    import numpy as _np
    import concourse.bacc as _bacc
    from concourse.bass_utils import run_bass_kernel_spmd as _run

    nc = _bacc.Bacc("TRN2", target_bir_lowering=False, num_devices=1)
    arrays, args = {}, []
    for name in _INS:
        a = _np.ascontiguousarray(inputs[name])
        arrays[f"in_{name}_dram"] = a
        args.append(nc.dram_tensor(f"in_{name}_dram", a.shape, mybir.dt.from_np(a.dtype), kind="ExternalInput").ap())
    shape = inputs["x"].shape
    args.append(nc.dram_tensor("out_dram", shape, F32, kind="ExternalOutput").ap())
    modulated_chain_kernel(nc, *args)
    r = _run(nc, [arrays], core_ids=[0])
    return r.results[0]["out_dram"]
```
